# Optimizing a Trainium2 kernel written in Bass

```python
import numpy as np
import jax
import jax.numpy as jnp

def _softmax(x, axis=-1):
    return jax.nn.softmax(x, axis=axis)

def _gelu(x):
    return jax.nn.gelu(x, approximate=True)

def _silu(x):
    return jax.nn.silu(x)

def _sigmoid(x):
    return jax.nn.sigmoid(x)

def _layernorm(x, axis=-1, eps=1e-05):
    m = jnp.mean(x, axis=axis, keepdims=True)
    v = jnp.var(x, axis=axis, keepdims=True)
    return (x - m) / jnp.sqrt(v + eps)

def _scatter_add(tgt, idx, src, axis=0):
    return tgt.at[idx].add(src)

def _segment_sum(src, seg, n):
    return jax.ops.segment_sum(src, seg, n)
kernel_name = 'mk_seq_preln_d1_jaxref_r4_0dc7e5'

def setup_inputs(seed: int=0):
    np.random.seed(seed)
    _w = jnp.asarray

    def _L0_attn_setup():
        import jax, jax.numpy as jnp
        import numpy as np
        import math
        HIDDEN = 512
        NUM_HEADS = 16
        NUM_KV_HEADS = 8
        HEAD_DIM = HIDDEN // NUM_HEADS
        ROPE_THETA = 1000000.0
        SPARSITY_RATIO = 0.5
        VISION_SPARSITY_RATIO = 0.4
        BATCH = 2
        SEQ = 512

        def rotate_half(x):
            h = x.shape[-1] // 2
            return jnp.concatenate([-x[..., h:], x[..., :h]], axis=-1)
        key = jax.random.key(seed)
        ks = jax.random.split(key, 12)
        s = 1.0 / math.sqrt(HIDDEN)
        return {'hidden_states': jax.random.normal(ks[0], (BATCH, SEQ, HIDDEN), jnp.float32), 'Wq': jax.random.normal(ks[1], (HIDDEN, NUM_HEADS * HEAD_DIM), jnp.float32) * s, 'bq': jax.random.normal(ks[2], (NUM_HEADS * HEAD_DIM,), jnp.float32) * 0.01, 'Wk': jax.random.normal(ks[3], (HIDDEN, NUM_KV_HEADS * HEAD_DIM), jnp.float32) * s, 'bk': jax.random.normal(ks[4], (NUM_KV_HEADS * HEAD_DIM,), jnp.float32) * 0.01, 'Wv': jax.random.normal(ks[5], (HIDDEN, NUM_KV_HEADS * HEAD_DIM), jnp.float32) * s, 'bv': jax.random.normal(ks[6], (NUM_KV_HEADS * HEAD_DIM,), jnp.float32) * 0.01, 'Wo': jax.random.normal(ks[7], (NUM_HEADS * HEAD_DIM, HIDDEN), jnp.float32) * s, 'bo': jax.random.normal(ks[8], (HIDDEN,), jnp.float32) * 0.01, 'Wr': jax.random.normal(ks[9], (HIDDEN, NUM_HEADS), jnp.float32) * s, 'br': jax.random.normal(ks[10], (NUM_HEADS,), jnp.float32) * 0.01}
    _L0_attn_in = _L0_attn_setup()

    def _L0_ffn_setup():
        import jax, jax.numpy as jnp
        import numpy as np
        B, T = (1, 128)
        DIM = 512
        MOE_INTER = 352
        N_EXPERTS = 64
        TOPK = 6
        N_SHARED = 2
        SHARED_INTER = N_SHARED * MOE_INTER
        CAPACITY = 128
        ROUTE_SCALE = 1.0
        key = jax.random.key(seed)
        ks = jax.random.split(key, 8)

        def w(k, shape, fan_in):
            return jax.random.normal(k, shape, jnp.float32) * fan_in ** (-0.5)
        return {'x': jax.random.normal(ks[0], (B, T, DIM), jnp.float32), 'gate_w': w(ks[1], (N_EXPERTS, DIM), DIM), 'w1': w(ks[2], (N_EXPERTS, MOE_INTER, DIM), DIM), 'w2': w(ks[3], (N_EXPERTS, DIM, MOE_INTER), MOE_INTER), 'w3': w(ks[4], (N_EXPERTS, MOE_INTER, DIM), DIM), 'sw1': w(ks[5], (SHARED_INTER, DIM), DIM), 'sw2': w(ks[6], (DIM, SHARED_INTER), SHARED_INTER), 'sw3': w(ks[7], (SHARED_INTER, DIM), DIM)}
    _L0_ffn_in = _L0_ffn_setup()
    _d = {'L0_attn_hidden_states': _L0_attn_in['hidden_states'], 'L0_attn_Wq': _L0_attn_in['Wq'], 'L0_attn_bq': _L0_attn_in['bq'], 'L0_attn_Wk': _L0_attn_in['Wk'], 'L0_attn_bk': _L0_attn_in['bk'], 'L0_attn_Wv': _L0_attn_in['Wv'], 'L0_attn_bv': _L0_attn_in['bv'], 'L0_attn_Wo': _L0_attn_in['Wo'], 'L0_attn_bo': _L0_attn_in['bo'], 'L0_attn_Wr': _L0_attn_in['Wr'], 'L0_attn_br': _L0_attn_in['br'], 'L0_ffn_gate_w': _L0_ffn_in['gate_w'], 'L0_ffn_w1': _L0_ffn_in['w1'], 'L0_ffn_w2': _L0_ffn_in['w2'], 'L0_ffn_w3': _L0_ffn_in['w3'], 'L0_ffn_sw1': _L0_ffn_in['sw1'], 'L0_ffn_sw2': _L0_ffn_in['sw2'], 'L0_ffn_sw3': _L0_ffn_in['sw3']}
    _x0 = _d['L0_attn_hidden_states']
    _d['L0_attn_hidden_states'] = jax.random.normal(jax.random.fold_in(jax.random.key(seed), 1), (4, 1024, 512), dtype=_x0.dtype)
    del _x0
    return _d

def reference(L0_attn_hidden_states, L0_attn_Wq, L0_attn_bq, L0_attn_Wk, L0_attn_bk, L0_attn_Wv, L0_attn_bv, L0_attn_Wo, L0_attn_bo, L0_attn_Wr, L0_attn_br, L0_ffn_gate_w, L0_ffn_w1, L0_ffn_w2, L0_ffn_w3, L0_ffn_sw1, L0_ffn_sw2, L0_ffn_sw3):

    def _L0_attn_ref(hidden_states, Wq, bq, Wk, bk, Wv, bv, Wo, bo, Wr, br):
        import jax, jax.numpy as jnp
        import numpy as np
        import math
        HIDDEN = 512
        NUM_HEADS = 16
        NUM_KV_HEADS = 8
        HEAD_DIM = HIDDEN // NUM_HEADS
        ROPE_THETA = 1000000.0
        SPARSITY_RATIO = 0.5
        VISION_SPARSITY_RATIO = 0.4
        BATCH = 2
        SEQ = 512

        def rotate_half(x):
            h = x.shape[-1] // 2
            return jnp.concatenate([-x[..., h:], x[..., :h]], axis=-1)
        bsz, q_len, _ = hidden_states.shape
        q = (hidden_states @ Wq + bq).reshape(bsz, q_len, NUM_HEADS, HEAD_DIM).transpose(0, 2, 1, 3)
        k = (hidden_states @ Wk + bk).reshape(bsz, q_len, NUM_KV_HEADS, HEAD_DIM).transpose(0, 2, 1, 3)
        v = (hidden_states @ Wv + bv).reshape(bsz, q_len, NUM_KV_HEADS, HEAD_DIM).transpose(0, 2, 1, 3)
        pos = jnp.arange(q_len, dtype=jnp.float32)
        inv_freq = 1.0 / ROPE_THETA ** (jnp.arange(0, HEAD_DIM, 2, dtype=jnp.float32) / HEAD_DIM)
        freqs = pos[:, None] * inv_freq[None, :]
        emb = jnp.concatenate([freqs, freqs], axis=-1)
        cos = jnp.cos(emb)[None, None, :, :]
        sin = jnp.sin(emb)[None, None, :, :]
        q = q * cos + rotate_half(q) * sin
        k = k * cos + rotate_half(k) * sin
        n_rep = NUM_HEADS // NUM_KV_HEADS
        k = jnp.repeat(k, n_rep, axis=1)
        v = jnp.repeat(v, n_rep, axis=1)
        routing = jax.nn.sigmoid(hidden_states @ Wr + br).transpose(0, 2, 1)
        ratio = VISION_SPARSITY_RATIO if q_len > 128 else SPARSITY_RATIO
        topk = max(1, min(int(q_len * ratio), q_len))
        _, idx = jax.lax.top_k(routing, topk)
        mask = jax.vmap(jax.vmap(lambda i: jnp.zeros((q_len,), bool).at[i].set(True)))(idx)
        scores = jnp.einsum('bhqd,bhkd->bhqk', q, k) / math.sqrt(HEAD_DIM)
        sparse = jnp.where(mask[:, :, None, :], scores, -jnp.inf)
        probs = jax.nn.softmax(sparse.astype(jnp.float32), axis=-1).astype(q.dtype)
        out = jnp.einsum('bhqk,bhkd->bhqd', probs, v)
        out = out.transpose(0, 2, 1, 3).reshape(bsz, q_len, NUM_HEADS * HEAD_DIM)
        return out @ Wo + bo

    def _L0_ffn_ref(x, gate_w, w1, w2, w3, sw1, sw2, sw3):
        import jax, jax.numpy as jnp
        import numpy as np
        B, T = (1, 128)
        DIM = 512
        MOE_INTER = 352
        N_EXPERTS = 64
        TOPK = 6
        N_SHARED = 2
        SHARED_INTER = N_SHARED * MOE_INTER
        CAPACITY = 128
        ROUTE_SCALE = 1.0
        Bb, Tt, D = x.shape
        xf = x.reshape(-1, D)
        N = xf.shape[0]
        logits = xf @ gate_w.T
        scores = jax.nn.softmax(logits, axis=-1)
        gate_vals, idx = jax.lax.top_k(scores, TOPK)
        gate_vals = gate_vals * ROUTE_SCALE
        E = gate_w.shape[0]
        fe = idx.reshape(-1)
        ft = jnp.repeat(jnp.arange(N), TOPK)
        onehot = (fe[:, None] == jnp.arange(E)[None, :]).astype(jnp.int32)
        pos = jnp.take_along_axis(jnp.cumsum(onehot, axis=0) - 1, fe[:, None], axis=1)[:, 0]
        keep = pos < CAPACITY
        buf = jnp.full((E, CAPACITY), N, dtype=jnp.int32)
        buf = buf.at[fe, pos].set(ft.astype(jnp.int32), mode='drop')
        xpad = jnp.concatenate([xf, jnp.zeros((1, D), xf.dtype)], axis=0)
        xe = xpad[buf]
        h = jax.nn.silu(jnp.einsum('ecd,eid->eci', xe, w1)) * jnp.einsum('ecd,eid->eci', xe, w3)
        ye = jnp.einsum('eci,edi->ecd', h, w2)
        pc = jnp.minimum(pos, CAPACITY - 1)
        op = ye[fe, pc] * keep[:, None].astype(ye.dtype)
        routed = (op * gate_vals.reshape(-1)[:, None]).reshape(N, TOPK, D).sum(axis=1)
        z = jax.nn.silu(xf @ sw1.T) * (xf @ sw3.T) @ sw2.T
        return (routed + z).reshape(Bb, Tt, D)
    x = L0_attn_hidden_states
    x = x + _L0_attn_ref(_layernorm(x, axis=-1), L0_attn_Wq, L0_attn_bq, L0_attn_Wk, L0_attn_bk, L0_attn_Wv, L0_attn_bv, L0_attn_Wo, L0_attn_bo, L0_attn_Wr, L0_attn_br)
    x = x + _L0_ffn_ref(_layernorm(x, axis=-1), L0_ffn_gate_w, L0_ffn_w1, L0_ffn_w2, L0_ffn_w3, L0_ffn_sw1, L0_ffn_sw2, L0_ffn_sw3)
    return x

_drawn_inputs = setup_inputs


def setup_inputs(seed=0):
    import zlib

    import numpy as np

    out = dict(_drawn_inputs(seed))
    spreads = {}
    factors = {'L0_attn_bq': 46.718, 'L0_attn_bk': 64.0, 'L0_attn_bv': 3.968, 'L0_attn_bo': 4.663}
    for name, (base, spread) in spreads.items():
        noise = np.random.default_rng([zlib.crc32(name.encode()), seed]).standard_normal(out[name].shape)
        drawn = base * np.exp(spread * noise) if base else spread * noise
        out[name] = jnp.asarray(drawn.astype(out[name].dtype))
    for name, factor in factors.items():
        out[name] = (out[name] * factor).astype(out[name].dtype)
    return out
```

```python
import math
from contextlib import ExitStack

import concourse.bass as bass
import concourse.mybir as mybir
from concourse.alu_op_type import AluOpType as ALU

ACT = mybir.ActivationFunctionType
F32, F32R, BF16, U32 = mybir.dt.float32, mybir.dt.float32r, mybir.dt.bfloat16, mybir.dt.uint32
AX_X = mybir.AxisListType.X

P = 128
B, S, D = 4, 1024, 512
N = B * S
HEADS, KV_HEADS, DH = 16, 8, 32
KD = D // P
HALF = 512
TILES = N // P
TOPK = int(S * 0.4)
EPS = 1e-5
EXPERTS, CHOSEN, CAPACITY, INTER = 64, 6, 128, 352
ROW = D + EXPERTS
SHARED = 704
SHARED_CHUNKS = -(-SHARED // P)


def normalise_and_route(nc, t):
    with ExitStack() as ctx:
        sb = lambda name, shape, dt=F32: ctx.enter_context(nc.sbuf_tensor(name, shape, dt))
        used = []

        def sem(name):
            used.append(ctx.enter_context(nc.semaphore(name)))
            return used[-1]

        x = sb("a_x", [P, 2, 4, D])
        xt = sb("a_xt", [P, 2, KD, HALF])
        stats = sb("a_stats", [P, 2, 4, 6])
        mv = sb("a_mv", [P, 2, 4, 2])
        sd = sb("a_sd", [P, 2, 4])
        rs = sb("a_rs", [P, 2, 4])
        eps = sb("a_eps", [P, 1])
        wr = sb("a_wr", [P, KD, HEADS])
        br = sb("a_br", [HEADS, 1])
        ident = sb("a_ident", [P, P])
        lg = sb("a_lg", [HEADS, 2, HALF])
        turned = [ctx.enter_context(nc.psum_tensor(f"a_turned{k}", [P, HALF], F32)) for k in range(KD)]
        logits = [ctx.enter_context(nc.psum_tensor(f"a_logits{u}", [P, HALF], F32)) for u in range(2)]
        consts = sem("a_consts")
        x_in = [sem(f"a_x_in{u}") for u in range(2)]
        eps_set = sem("a_eps_set")
        stat_step = sem("a_stat_step")
        aggregated = sem("a_aggregated")
        rooted = sem("a_rooted")
        inverted = sem("a_inverted")
        normed = sem("a_normed")
        turned_done = sem("a_turned_done")
        evacuated = sem("a_evacuated")
        logits_done = sem("a_logits_done")
        logits_out = sem("a_logits_out")
        xt_stored = [sem(f"a_xt_stored{u}") for u in range(2)]
        lg_stored = [sem(f"a_lg_stored{u}") for u in range(2)]
        block = ctx.enter_context(nc.Block())

        @block.sync
        def _(sp):
            sp.dma_start(wr[:], t["wr"].rearrange("(k p) h -> p k h", p=P)).then_inc(consts, 16)
            sp.dma_start(br[:], t["br"].rearrange("(h o) -> h o", o=1)).then_inc(consts, 16)
            sp.dma_start(ident[:], t["ident"]).then_inc(consts, 16)
            for u in range(2):
                sp.dma_start(x[:, u], t["x"][0, u * HALF:(u + 1) * HALF].rearrange("(t p) d -> p t d", p=P)).then_inc(x_in[u], 16)
            with sp.Fori(1, B) as b:
                for u in range(2):
                    sp.wait_ge(turned_done, 8 * b + 4 * u - 4)
                    sp.dma_start(x[:, u], t["x"][b, u * HALF:(u + 1) * HALF].rearrange("(t p) d -> p t d", p=P)).then_inc(x_in[u], 16)

        @block.vector
        def _(dve):
            nc.vector.memset(eps[:], EPS).then_inc(eps_set, 1)
            with dve.Fori(0, B) as b:
                for u in range(2):
                    dve.sem_clear(stat_step)
                    dve.wait_ge(x_in[u], 16 * b + 16)
                    for j in range(4):
                        nc.vector.bn_stats(stats[:, u, j], x[:, u, j]).then_inc(stat_step, 1)
                    for j in range(4):
                        dve.wait_ge(stat_step, j + 1)
                        nc.vector.bn_aggr(mv[:, u, j], stats[:, u, j]).then_inc(aggregated, 1)
                    dve.wait_ge(rooted, 2 * b + u + 1)
                    nc.vector.reciprocal(rs[:, u], sd[:, u]).then_inc(inverted, 1)
                    dve.wait_ge(inverted, 2 * b + u + 1)
                    for j in range(4):
                        nc.vector.tensor_scalar(x[:, u, j], x[:, u, j], mv[:, u, j, 0:1], rs[:, u, j:j + 1],
                                                ALU.subtract, ALU.mult).then_inc(normed, 1)

        @block.scalar
        def _(act):
            act.wait_ge(eps_set, 1)
            act.wait_ge(consts, 48)

            def finish(b, u):
                for k in range(KD):
                    act.wait_ge(turned_done, 8 * b + 4 * u + k + 1)
                    nc.scalar.copy(xt[:, u, k], turned[k][:]).then_inc(evacuated, 1)
                act.wait_ge(evacuated, 8 * b + 4 * u + 4)
                act.dma_start(t["xnt"][2 * b + u], xt[:, u]).then_inc(xt_stored[u], 16)
                act.wait_ge(logits_done, 2 * b + u + 1)
                nc.scalar.activation(lg[:, u], logits[u][0:HEADS, :], ACT.Identity, bias=br[:, 0:1]).then_inc(logits_out, 1)
                act.wait_ge(logits_out, 2 * b + u + 1)
                act.dma_start(t["lg"][b, :, u * HALF:(u + 1) * HALF], lg[:, u]).then_inc(lg_stored[u], 16)

            def root(b, u):
                act.wait_ge(aggregated, 8 * b + 4 * u + 4)
                nc.scalar.activation(sd[:, u], mv[:, u, :, 1], ACT.Sqrt, bias=eps[:, 0:1]).then_inc(rooted, 1)

            for u in range(2):
                root(0, u)
                finish(0, u)
            with act.Fori(1, B) as b:
                for u in range(2):
                    root(b, u)
                    act.wait_ge(xt_stored[u], 16 * b)
                    act.wait_ge(lg_stored[u], 16 * b)
                    finish(b, u)
            for u in range(2):
                act.wait_ge(xt_stored[u], 16 * B)
                act.wait_ge(lg_stored[u], 16 * B)

        @block.tensor
        def _(pe):
            pe.wait_ge(consts, 48)

            def turn(b, u, first):
                pe.wait_ge(normed, 8 * b + 4 * u + 4)
                for k in range(KD):
                    if not first:
                        pe.wait_ge(evacuated, 8 * b + 4 * u + k - 3)
                    for j in range(4):
                        last = nc.tensor.transpose(turned[k][:, j * P:(j + 1) * P], x[:, u, j, k * P:(k + 1) * P], ident[:])
                    last.then_inc(turned_done, 1)
                for k in range(KD):
                    pe.wait_ge(evacuated, 8 * b + 4 * u + k + 1)
                    last = nc.tensor.matmul(logits[u][0:HEADS, :], wr[:, k], xt[:, u, k], start=(k == 0), stop=(k == KD - 1))
                last.then_inc(logits_done, 1)

            turn(0, 0, True)
            turn(0, 1, False)
            with pe.Fori(1, B) as b:
                for u in range(2):
                    pe.wait_ge(logits_out, 2 * b + u - 1)
                    turn(b, u, False)
    return used


def project_and_rank(nc, t):
    QK = (HEADS + KV_HEADS) * DH
    ROWS = B * HEADS
    ROUNDS = -(-TOPK // 8)
    with ExitStack() as ctx:
        sb = lambda name, shape, dt=F32: ctx.enter_context(nc.sbuf_tensor(name, shape, dt))
        sem = lambda name: ctx.enter_context(nc.semaphore(name))
        w = sb("b_w", [P, KD, 2 * D])
        wh = sb("b_wh", [P, KD, 2 * D], F32R)
        wl = sb("b_wl", [P, KD, 2 * D], F32R)
        bias = sb("b_bias", [1, 2 * D])
        rest = sb("b_rest", [1, 2, 2 * D])
        part = sb("b_part", [1, 2, 2 * D], BF16)
        bias3 = sb("b_bias3", [P, 2 * D], BF16)
        ones = sb("b_ones", [P, P], BF16)
        ident = sb("b_ident", [P, P])
        x = sb("b_x", [P, 2, KD, P])
        xh = sb("b_xh", [P, 2, KD, P], F32R)
        xl = sb("b_xl", [P, 2, KD, P], F32R)
        cs = sb("b_cs", [P, 2, 2, DH])
        qk = sb("b_qk", [P, 2, QK])
        qkc = sb("b_qkc", [P, QK])
        qks = sb("b_qks", [P, QK])
        rot = sb("b_rot", [P, 2, QK])
        kvrow = sb("b_kvrow", [P, 2, KV_HEADS, 4 * DH])
        qt = sb("b_qt", [P, 2, HEADS * DH])
        qh = sb("b_qh", [P, 2, HEADS * DH], F32R)
        ql = sb("b_ql", [P, 2, HEADS * DH], F32R)
        lg = sb("b_lg", [ROWS, S])
        top = sb("b_top", [ROWS, 8])
        at = sb("b_at", [ROWS, 8], U32)
        keys = sb("b_keys", [ROWS, ROUNDS * 8], U32)
        psum = lambda name: ctx.enter_context(nc.psum_tensor(name, [P, 512], F32))
        pq = [psum(f"b_pq{u}") for u in range(2)]
        pkv = [psum(f"b_pkv{u}") for u in range(2)]
        pt = [psum(f"b_pt{u}") for u in range(2)]
        w_in, bias_in, lg_in, ident_in = sem("b_w_in"), sem("b_bias_in"), sem("b_lg_in"), sem("b_ident_in")
        zeroed, bias_step, rows_in = sem("b_zeroed"), sem("b_bias_step"), sem("b_rows_in")
        wh_done, wl_done = sem("b_wh_done"), sem("b_wl_done")
        x_in = [sem(f"b_x_in{u}") for u in range(2)]
        cs_in = [sem(f"b_cs_in{u}") for u in range(2)]
        xh_done, xl_done = sem("b_xh_done"), sem("b_xl_done")
        projected, copied, v_copied = sem("b_projected"), sem("b_copied"), sem("b_v_copied")
        multiplied, rotated = sem("b_multiplied"), sem("b_rotated")
        turned, qt_done, kh_done = sem("b_turned"), sem("b_qt_done"), sem("b_kh_done")
        ql_done, kl_done = sem("b_ql_done"), sem("b_kl_done")
        q_stored = [sem(f"b_q_stored{u}") for u in range(2)]
        kv_stored = [sem(f"b_kv_stored{u}") for u in range(2)]
        ranked, kept, keys_stored = sem("b_ranked"), sem("b_kept"), sem("b_keys_stored")
        block = ctx.enter_context(nc.Block())
        xnt = t["xnt"].rearrange("a p k (j c) -> a j p k c", c=P)
        kv = t["kv"].rearrange("(n p h) c -> n p h c", p=P, h=KV_HEADS)

        def tile(i, u):
            return i // 4, 2 * (i % 4) + u

        @block.sync
        def _(sp):
            sp.dma_start(w[:, :, 0:D], t["wq"].rearrange("(k p) n -> p k n", p=P)).then_inc(w_in, 16)
            sp.dma_start(w[:, :, D:D + D // 2], t["wk"].rearrange("(k p) n -> p k n", p=P)).then_inc(w_in, 16)
            sp.dma_start(w[:, :, D + D // 2:], t["wv"].rearrange("(k p) n -> p k n", p=P)).then_inc(w_in, 16)
            row = lambda a: a.rearrange("(o n) -> o n", o=1)
            sp.dma_start(bias[:, 0:D], row(t["bq"])).then_inc(bias_in, 16)
            sp.dma_start(bias[:, D:D + D // 2], row(t["bk"])).then_inc(bias_in, 16)
            sp.dma_start(bias[:, D + D // 2:], row(t["bv"])).then_inc(bias_in, 16)
            sp.dma_start(ident[:], t["ident"]).then_inc(ident_in, 16)
            sp.dma_start(lg[:], t["lg"].rearrange("b h s -> (b h) s")).then_inc(lg_in, 16)

            def load_x(i, u):
                sp.dma_start(x[:, u], xnt[i // 2, 2 * (i % 2) + u]).then_inc(x_in[u], 16)

            def load_cs(i, u):
                sp.dma_start(cs[:, u], t["cs"][tile(i, u)[1]]).then_inc(cs_in[u], 16)

            def store(i, u):
                b, j = tile(i, u)
                sp.wait_ge(ql_done, 2 * i + u + 1)
                for name, src in (("qh", qh), ("ql", ql)):
                    sp.dma_start(t[name][b, :, j].rearrange("g p c -> p g c"),
                                 src[:, u].bitcast(F32).rearrange("p (g c) -> p g c", c=P)).then_inc(q_stored[u], 16)
                sp.wait_ge(kl_done, 2 * i + u + 1)
                sp.wait_ge(v_copied, 2 * i + u + 1)
                sp.dma_start(kv[2 * i + u], kvrow[:, u]).then_inc(kv_stored[u], 16)

            def step(i, last=0):
                if last != 1:
                    sp.wait_ge(xl_done, 2 * i + 2)
                    load_x(i + 1, 1)
                    sp.wait_ge(multiplied, 4 * i + 2)
                    load_cs(i + 1, 0)
                if not (isinstance(i, int) and i == 0):
                    store(i - 1, 1)
                if not last:
                    sp.wait_ge(xl_done, 2 * i + 3)
                    load_x(i + 2, 0)
                if last != 1:
                    sp.wait_ge(multiplied, 4 * i + 4)
                    load_cs(i + 1, 1)
                store(i, 0)

            for u in range(2):
                load_x(0, u)
                load_cs(0, u)
            sp.wait_ge(xl_done, 1)
            load_x(1, 0)
            step(0)
            with sp.Fori(1, TILES // 2 - 2) as i:
                step(i)
            step(TILES // 2 - 2, last=2)
            step(TILES // 2 - 1, last=1)
            store(TILES // 2 - 1, 1)
            sp.wait_ge(kept, 1)
            sp.dma_start(t["keys"], keys[:]).then_inc(keys_stored, 16)
            for u in range(2):
                sp.wait_ge(q_stored[u], 32 * (TILES // 2))
                sp.wait_ge(kv_stored[u], 16 * (TILES // 2))
            sp.wait_ge(keys_stored, 16)

        @block.vector
        def _(dve):
            nc.vector.memset(bias3[:], 0.0).then_inc(zeroed, 1)
            nc.vector.memset(ones[:], 1.0).then_inc(zeroed, 1)
            dve.wait_ge(bias_in, 48)
            dve.wait_ge(zeroed, 2)
            nc.vector.tensor_copy(bias3[0:1, :], bias[:]).then_inc(bias_step, 1)
            dve.wait_ge(bias_step, 1)
            nc.vector.tensor_tensor(rest[:, 0], bias[:], bias3[0:1, :], ALU.subtract).then_inc(bias_step, 1)
            dve.wait_ge(bias_step, 2)
            nc.vector.tensor_copy(part[:, 0], rest[:, 0]).then_inc(bias_step, 1)
            dve.wait_ge(bias_step, 3)
            nc.vector.tensor_tensor(rest[:, 1], rest[:, 0], part[:, 0], ALU.subtract).then_inc(bias_step, 1)
            dve.wait_ge(bias_step, 4)
            nc.vector.tensor_copy(part[:, 1], rest[:, 1]).then_inc(bias_step, 1)
            for k in range(KD):
                dve.wait_ge(wh_done, k + 1)
                nc.vector.tensor_tensor(wl[:, k], w[:, k], wh[:, k].bitcast(F32), ALU.subtract).then_inc(wl_done, 1)
            dve.wait_ge(lg_in, 16)

            def rank(r):
                dve.sem_clear(ranked)
                nc.vector.max(top[:], lg[:]).then_inc(ranked, 1)
                dve.wait_ge(ranked, 1)
                nc.vector.max_index(at[:], top[:], lg[:]).then_inc(ranked, 1)
                dve.wait_ge(ranked, 2)
                nc.vector.match_replace(lg[:], top[:], lg[:], -3e38).then_inc(ranked, 1)
                nc.vector.tensor_copy(keys[:, bass.ds(8 * r, 8)], at[:]).then_inc(ranked, 1)
                dve.wait_ge(ranked, 4)

            def split(i, u, first=False):
                dve.wait_ge(xh_done, 2 * i + u + 1)
                if not first:
                    dve.wait_ge(projected, 4 * i + 2 * u - 2)
                nc.vector.tensor_tensor(xl[:, u], x[:, u], xh[:, u].bitcast(F32), ALU.subtract).then_inc(xl_done, 1)

            def finish(i, u):
                dve.wait_ge(qt_done, 4 * i + 2 * u + 2)
                nc.vector.tensor_tensor(ql[:, u], qt[:, u], qh[:, u].bitcast(F32), ALU.subtract).then_inc(ql_done, 1)

            def step(i, r=None):
                for u in range(2):
                    split(i + 1, u)
                    if r is not None:
                        rank(r + 2 * u)
                    finish(i, u)
                    if r is not None:
                        rank(r + 2 * u + 1)

            split(0, 0, True)
            split(0, 1, True)
            with dve.Fori(0, ROUNDS // 4) as i:
                step(i, 4 * i)
            for i in range(ROUNDS // 4, TILES // 2 - 1):
                step(i)
            finish(TILES // 2 - 1, 0)
            finish(TILES // 2 - 1, 1)
            nc.vector.tensor_copy(keys[:, TOPK:], keys[:, TOPK - 1:TOPK].broadcast_to([ROWS, ROUNDS * 8 - TOPK])).then_inc(kept, 1)

        @block.scalar
        def _(act):
            act.wait_ge(w_in, 48)
            for k in range(KD):
                nc.scalar.copy(wh[:, k], w[:, k]).then_inc(wh_done, 1)
            for r in range(2):
                act.wait_ge(bias_step, 3 + 2 * r)
                act.dma_start(bias3[1 + r:2 + r, :], part[:, r]).then_inc(rows_in, 16)

            def split(i, u, first=False):
                act.wait_ge(x_in[u], 16 * i + 16)
                if not first:
                    act.wait_ge(projected, 4 * i + 2 * u - 2)
                nc.scalar.copy(xh[:, u], x[:, u]).then_inc(xh_done, 1)

            def copy_out(i, u, first=False):
                act.wait_ge(projected, 4 * i + 2 * u + 1)
                if not first:
                    act.wait_ge(multiplied, 4 * i + 2 * u - 2)
                nc.scalar.copy(qk[:, u, 0:D], pq[u][:]).then_inc(copied, 1)
                act.wait_ge(projected, 4 * i + 2 * u + 2)
                nc.scalar.copy(qk[:, u, D:QK], pkv[u][:, 0:D // 2]).then_inc(copied, 1)
                if not first:
                    act.wait_ge(kv_stored[u], 16 * i)
                nc.scalar.copy(kvrow[:, u, :, 3 * DH:], pkv[u][:, D // 2:].rearrange("p (h c) -> p h c", c=DH)).then_inc(v_copied, 1)

            def finish(i, u, first=False):
                act.wait_ge(turned, 2 * i + u + 1)
                if not first:
                    act.wait_ge(q_stored[u], 32 * i)
                nc.scalar.copy(qt[:, u], pt[u][:]).then_inc(qt_done, 1)
                nc.scalar.copy(qh[:, u], pt[u][:]).then_inc(qt_done, 1)
                act.wait_ge(rotated, 4 * i + 2 * u + 2)
                k = rot[:, u, D:QK].rearrange("p (h o c) -> p h o c", o=1, c=DH)
                nc.scalar.copy(kvrow[:, u, :, 0:2 * DH].rearrange("p h (o c) -> p h o c", c=DH).bitcast(F32R),
                               k.broadcast_to([P, KV_HEADS, 2, DH])).then_inc(kh_done, 1)

            split(0, 0, True)
            split(0, 1, True)
            copy_out(0, 0, True)
            split(1, 0)
            copy_out(0, 1, True)
            finish(0, 0, True)
            split(1, 1)
            copy_out(1, 0)
            finish(0, 1, True)
            with act.Fori(1, TILES // 2 - 1) as i:
                split(i + 1, 0)
                copy_out(i, 1)
                finish(i, 0)
                split(i + 1, 1)
                copy_out(i + 1, 0)
                finish(i, 1)
            last = TILES // 2 - 1
            copy_out(last, 1)
            finish(last, 0)
            finish(last, 1)

        @block.gpsimd
        def _(pool):
            def rotate(i, u, first=False, second=False):
                pool.wait_ge(copied, 4 * i + 2 * u + 2)
                pool.wait_ge(cs_in[u], 16 * i + 16)
                if not first:
                    pool.wait_ge(rotated, 4 * i + 2 * u)
                heads = lambda a: a.rearrange("p (h c) -> p h c", c=DH)
                src = heads(qk[:, u])
                table = lambda n: cs[:, u, n:n + 1, :].broadcast_to([P, HEADS + KV_HEADS, DH])
                nc.gpsimd.tensor_tensor(heads(qkc[:]), src, table(0), ALU.mult).then_inc(multiplied, 1)
                nc.gpsimd.tensor_tensor(heads(qks[:]), src, table(1), ALU.mult).then_inc(multiplied, 1)
                pool.wait_ge(multiplied, 4 * i + 2 * u + 2)
                if not (first or second):
                    pool.wait_ge(turned, 2 * i + u - 1)
                    pool.wait_ge(kl_done, 2 * i + u - 1)
                for a, b in ((0, DH // 2), (DH // 2, 0)):
                    nc.gpsimd.tensor_tensor(heads(rot[:, u])[:, :, a:a + DH // 2], heads(qkc[:])[:, :, a:a + DH // 2],
                                            heads(qks[:])[:, :, b:b + DH // 2], ALU.add).then_inc(rotated, 1)

            def finish(i, u):
                pool.wait_ge(kh_done, 2 * i + u + 1)
                nc.gpsimd.tensor_tensor(kvrow[:, u, :, 2 * DH:3 * DH].bitcast(F32R), rot[:, u, D:QK].rearrange("p (h c) -> p h c", c=DH),
                                        kvrow[:, u, :, 0:DH], ALU.subtract).then_inc(kl_done, 1)

            rotate(0, 0, first=True)
            rotate(0, 1, second=True)
            finish(0, 0)
            rotate(1, 0)
            finish(0, 1)
            with pool.Fori(1, TILES // 2 - 1) as i:
                rotate(i, 1)
                finish(i, 0)
                rotate(i + 1, 0)
                finish(i, 1)
            last = TILES // 2 - 1
            rotate(last, 1)
            finish(last, 0)
            finish(last, 1)

        @block.tensor
        def _(pe):
            def project(i, u, first=False):
                pe.wait_ge(xl_done, 2 * i + u + 1)
                for n, out in enumerate((pq[u], pkv[u])):
                    if not first:
                        if n == 0:
                            pe.wait_ge(copied, 4 * i + 2 * u - 3)
                        else:
                            pe.wait_ge(v_copied, 2 * i + u - 1)
                    cols = slice(n * D, (n + 1) * D)
                    nc.tensor.matmul(out[:], ones[:], bias3[:, cols], start=True, stop=False)
                    for k in range(KD):
                        nc.tensor.matmul(out[:], xh[:, u, k], wh[:, k, cols], start=False, stop=False)
                        nc.tensor.matmul(out[:], xh[:, u, k], wl[:, k, cols], start=False, stop=False)
                        last = nc.tensor.matmul(out[:], xl[:, u, k], wh[:, k, cols], start=False, stop=(k == KD - 1))
                    last.then_inc(projected, 1)

            def turn(i, u, first=False):
                pe.wait_ge(rotated, 4 * i + 2 * u + 2)
                if not first:
                    pe.wait_ge(qt_done, 4 * i + 2 * u - 2)
                for g in range(4):
                    last = nc.tensor.transpose(pt[u][:, g * P:(g + 1) * P], rot[:, u, g * P:(g + 1) * P], ident[:])
                last.then_inc(turned, 1)

            pe.wait_ge(ident_in, 16)
            pe.wait_ge(rows_in, 32)
            pe.wait_ge(wl_done, KD)
            pe.wait_ge(bias_step, 1)
            project(0, 0, True)
            project(0, 1, True)
            turn(0, 0, True)
            project(1, 0)
            turn(0, 1, True)
            with pe.Fori(1, TILES // 2 - 1) as i:
                project(i, 1)
                turn(i, 0)
                project(i + 1, 0)
                turn(i, 1)
            last = TILES // 2 - 1
            project(last, 1)
            turn(last, 0)
            turn(last, 1)


def attend(nc, t):
    ROWS = B * HEADS
    SLOTS = -(-TOPK // 8) * 8
    FULL = TOPK // P
    LAST = TOPK - FULL * P
    PIECES = 4 * FULL + 1
    GROUPS = ROWS // 4
    PARTS = 3 * DH
    MAXROW = PARTS
    MAX_AT, SUMS_AT = 22, 14
    DEEP = MAXROW + 8
    PAD = SLOTS
    KTW = 640
    TURNS = 7
    STEPS = 2 * PIECES
    NE = 4
    SCALE = 1.0 / math.sqrt(DH)
    with ExitStack() as ctx:
        sb = lambda name, shape, dt=F32: ctx.enter_context(nc.sbuf_tensor(name, shape, dt))
        sem = lambda name: ctx.enter_context(nc.semaphore(name))
        psum = lambda name: ctx.enter_context(nc.psum_tensor(name, [P, 512], F32))
        ident = sb("c_ident", [P, P])
        keyu = sb("c_keyu", [ROWS, SLOTS], U32)
        keyf = sb("c_keyf", [ROWS, SLOTS])
        base = sb("c_base", [ROWS, 1])
        rowidx = sb("c_rowidx", [P, GROUPS, PIECES], U32)
        picked = sb("c_picked", [P, 2, PIECES], U32)
        rows = sb("c_rows", [P, 2, PIECES, P])
        pick_rows = sb("c_pick_rows", [P, 4, KTW])
        kt = sb("c_kt", [P, 2, 4, KTW], F32R)
        q = sb("c_q", [P, 2, 4, S], F32R)
        mx = sb("c_mx", [P, 8, 4])
        neg = sb("c_neg", [P, 8, 4])
        ma = sb("c_ma", [P, 8, DEEP])
        mrow = sb("c_mrow", [P, 2, S], F32R)
        e = sb("c_e", [P, NE, HALF])
        ones = sb("c_ones", [P, DH])
        ones_last = sb("c_ones_last", [P, 4, DH])
        v = sb("c_v", [P, 2, PIECES - 1, DH])
        v_last = sb("c_v_last", [P, 2, 4, DH])
        sums = sb("c_sums", [P, HALF])
        inv = sb("c_inv", [P, 4 * HALF // P])
        wide = sb("c_wide", [P, HALF])
        att = sb("c_att", [P, 2, S])
        ps = [psum(f"c_ps{n}") for n in range(2)]
        pmix = [psum(f"c_pmix{n}") for n in range(3)]
        pout = psum("c_pout")
        psum_e = [psum(f"c_psum{n}") for n in range(2)]
        consts, set_up, keyf_step, key_turned, indexed = (sem(f"c_{n}") for n in ("consts", "set_up", "keyf_step", "key_turned", "indexed"))
        picked_done = sem("c_picked_done")
        gathered = [sem(f"c_gathered{s}") for s in range(2)]
        q_in = [sem(f"c_q_in{s}") for s in range(2)]
        m_in = [sem(f"c_m_in{s}") for s in range(2)]
        v_padded, v_moved, turned, emptied = sem("c_v_padded"), sem("c_v_moved"), sem("c_turned"), sem("c_emptied")
        s1_done, s1_read, negated, ma_done = sem("c_s1_done"), sem("c_s1_read"), sem("c_negated"), sem("c_ma_done")
        s2_done, exp_done, pv_done, att_done = (sem(f"c_{n}") for n in ("s2_done", "exp_done", "pv_done", "att_done"))
        sums_out, out_copied, sums_turned, inverted, spread = (sem(f"c_{n}") for n in ("sums_out", "out_copied", "sums_turned", "inverted", "spread"))
        att_stored = [sem(f"c_att_stored{s}") for s in range(2)]
        block = ctx.enter_context(nc.Block())
        q_dram = {n: t[n].rearrange("b g j p c -> (b g) j p c") for n in ("qh", "ql")}
        att_dram = t["att"].rearrange("b g p s -> (b g) p s")
        MEMSETS = 5 + 4

        @block.sync
        def _(sp):
            sp.dma_start(keyu[:], t["keys"]).then_inc(consts, 16)
            sp.dma_start(base[:], t["kv_base"]).then_inc(consts, 16)
            sp.dma_start(ident[:], t["ident"]).then_inc(consts, 16)
            sp.dma_start(pick_rows[MAXROW:P], t["pick_rows"]).then_inc(consts, 16)

            def load_q(i, s):
                for j in range(4):
                    for part, name in enumerate(("qh", "ql", "qh")):
                        sp.dma_start(q[part * DH:(part + 1) * DH, s, j].bitcast(F32).rearrange("p (t c) -> p t c", c=P),
                                     q_dram[name][2 * i + s, :, j * DH:(j + 1) * DH].rearrange("t p c -> p t c")).then_inc(q_in[s], 16)

            def load_max(i, s):
                sp.wait_ge(emptied, TURNS * (2 * i + s) + TURNS)
                sp.dma_start(q[MAXROW:DEEP, s].bitcast(F32),
                             mrow[MAXROW:DEEP, s].bitcast(F32).rearrange("p (o c) -> p o c", o=1).broadcast_to([DEEP - MAXROW, 4, S])).then_inc(m_in[s], 16)

            def store(i, s):
                sp.wait_ge(att_done, 4 * i + 2 * s + 2)
                sp.dma_start(att_dram[2 * i + s], att[:, s]).then_inc(att_stored[s], 16)

            load_q(0, 0)
            load_q(0, 1)
            load_max(0, 0)
            with sp.Fori(0, GROUPS // 2 - 1) as i:
                load_max(i, 1)
                sp.wait_ge(s2_done, STEPS * (2 * i + 1))
                load_q(i + 1, 0)
                store(i, 0)
                load_max(i + 1, 0)
                sp.wait_ge(s2_done, STEPS * (2 * i + 2))
                load_q(i + 1, 1)
                store(i, 1)
            last = GROUPS // 2 - 1
            load_max(last, 1)
            store(last, 0)
            store(last, 1)
            for s in range(2):
                sp.wait_ge(att_stored[s], 16 * (GROUPS // 2))

        @block.gpsimd
        def _(pool):
            nc.gpsimd.memset(kt[:].bitcast(F32), 0.0).then_inc(set_up, 1)
            nc.gpsimd.memset(ma[:], 0.0).then_inc(set_up, 1)
            nc.gpsimd.memset(ones[:], 1.0).then_inc(set_up, 1)
            nc.gpsimd.memset(ones_last[:], 0.0).then_inc(set_up, 1)
            nc.gpsimd.memset(v_last[:], 0.0).then_inc(set_up, 1)
            pool.wait_ge(set_up, 5)
            for j in range(4):
                nc.gpsimd.memset(ones_last[j * DH:j * DH + LAST, j], 1.0).then_inc(set_up, 1)
            pool.wait_ge(indexed, FULL + 4)

            def gather(i, s, waits=True):
                pool.sem_clear(picked_done)
                if waits:
                    pool.wait_ge(turned, TURNS * (2 * i + s - 2) + 5)
                    pool.wait_ge(v_moved, 2 * i + s - 1)
                group = pool.snap(2 * i + s)
                nc.gpsimd.tensor_copy(picked[:, s], rowidx[:, group]).then_inc(picked_done, 1)
                pool.wait_ge(picked_done, 1)
                for n in range(PIECES):
                    nc.gpsimd.indirect_dma_start(rows[:, s, n], None, t["kv"], bass.IndirectOffsetOnAxis(picked[:, s, n:n + 1], 0)).then_inc(gathered[s], 16)

            gather(0, 0, False)
            gather(0, 1, False)
            with pool.Fori(1, GROUPS // 2) as i:
                gather(i, 0)
                gather(i, 1)

        TURN_AT = 2 * SUMS_AT - 6
        SPREAD_AT = TURN_AT + 4

        @block.vector
        def _(dve):
            dve.wait_ge(consts, 64)
            nc.vector.tensor_copy(keyf[:], keyu[:]).then_inc(keyf_step, 1)
            dve.wait_ge(keyf_step, 1)
            nc.vector.tensor_scalar(keyf[:], keyf[:], float(KV_HEADS), base[:, 0:1], ALU.mult, ALU.add).then_inc(keyf_step, 1)
            dve.wait_ge(set_up, MEMSETS)
            for s in range(2):
                nc.vector.tensor_copy(kt[MAXROW:P, s], pick_rows[MAXROW:P]).then_inc(keyf_step, 1)
            dve.wait_ge(key_turned, 1)
            for c in range(FULL):
                nc.vector.tensor_copy(rowidx[:, :, c:4 * FULL:FULL], pout[:, c * ROWS:(c + 1) * ROWS].rearrange("p (g j) -> p g j", j=4)).then_inc(indexed, 1)
            for j in range(4):
                nc.vector.tensor_copy(rowidx[j * DH:(j + 1) * DH, :, PIECES - 1],
                                      pout[0:DH, FULL * ROWS:(FULL + 1) * ROWS].rearrange("p (g j) -> p g j", j=4)[:, :, j]).then_inc(indexed, 1)

            def move_v(i, s):
                dve.wait_ge(gathered[s], 16 * PIECES * (i + 1))
                nc.vector.tensor_copy(v[:, s], rows[:, s, 0:PIECES - 1, PARTS:]).then_inc(v_padded, 1)
                for j in range(4):
                    nc.vector.tensor_copy(v_last[j * DH:j * DH + LAST, s, j], rows[j * DH:j * DH + LAST, s, PIECES - 1, PARTS:]).then_inc(v_moved if j == 3 else v_padded, 1)

            def maxima(i, s, n0, n1):
                for n in range(n0, n1):
                    dve.wait_ge(s1_done, 32 * (2 * i + s) + n + 1)
                    nc.vector.tensor_reduce(mx[:, n % 8, n // 8:n // 8 + 1], pmix[(5 + n) % 3][:, 0:SLOTS], AX_X, ALU.max).then_inc(s1_read, 1)

            def negate(i, s, first=False):
                g = 2 * i + s
                dve.wait_ge(s1_read, 32 * g + 32)
                nc.vector.tensor_scalar(neg[:], mx[:], -1.0, None, ALU.mult).then_inc(negated, 1)
                dve.wait_ge(negated, 2 * g + 1)
                if not first:
                    dve.wait_ge(turned, TURNS * g)
                nc.vector.tensor_copy(ma[:, :, MAXROW:DEEP:2].bitcast(F32R), neg[:]).then_inc(negated, 1)
                dve.wait_ge(negated, 2 * g + 2)
                nc.vector.tensor_tensor(ma[:, :, MAXROW + 1:DEEP:2], neg[:], ma[:, :, MAXROW:DEEP:2], ALU.subtract).then_inc(ma_done, 1)

            def invert(i, s, half):
                g = 2 * i + s
                dve.wait_ge(sums_turned, 2 * g + half + 1)
                nc.vector.reciprocal(inv[:], psum_e[half][:, 0:4 * HALF // P]).then_inc(inverted, 1)
                dve.wait_ge(inverted, 3 * (2 * g + half) + 1)
                for k in range(2):
                    here, there = slice(2 * k, 2 * k + 2), slice(2 - 2 * k, 4 - 2 * k)
                    nc.vector.tensor_copy(wide[:].rearrange("p (c j o) -> p c j o", j=4, o=DH)[:, :, here],
                                          inv[:].rearrange("p (c j o) -> p c j o", j=4, o=1)[:, :, there].broadcast_to([P, HALF // P, 2, DH])).then_inc(inverted, 1)

            def normalise(i, s, half):
                g = 2 * i + s
                dve.wait_ge(out_copied, 2 * g + half + 1)
                dve.wait_ge(spread, 2 * g + half + 1)
                rows = att[:, s, half * HALF:(half + 1) * HALF]
                nc.vector.tensor_tensor(rows, rows, psum_e[half][:], ALU.mult).then_inc(att_done, 1)

            def group(i, s, nxt, before):
                if before:
                    invert(*before, 1)
                if nxt:
                    move_v(*nxt)
                    maxima(*nxt, 0, 2)
                if before:
                    normalise(*before, 1)
                if nxt:
                    maxima(*nxt, 2, TURN_AT)
                invert(i, s, 0)
                if nxt:
                    maxima(*nxt, TURN_AT, SPREAD_AT)
                normalise(i, s, 0)
                if nxt:
                    maxima(*nxt, SPREAD_AT, 32)
                    negate(*nxt)

            move_v(0, 0)
            maxima(0, 0, 0, 32)
            negate(0, 0, True)
            group(0, 0, (0, 1), None)
            group(0, 1, (1, 0), (0, 0))
            with dve.Fori(1, GROUPS // 2 - 1) as i:
                group(i, 0, (i, 1), (i - 1, 1))
                group(i, 1, (i + 1, 0), (i, 0))
            last = GROUPS // 2 - 1
            group(last, 0, (last, 1), (last - 1, 1))
            group(last, 1, None, (last, 0))
            invert(last, 1, 1)
            normalise(last, 1, 1)

        @block.scalar
        def _(act):
            def empty_k(i, s, n, first=False):
                g = 2 * i + s
                if n == 0 and not first:
                    act.wait_ge(s2_done, STEPS * (g - 1))
                act.wait_ge(turned, TURNS * g + n + 1)
                bank = pmix[n % 3]
                if n < 4:
                    nc.scalar.copy(kt[0:PARTS, s, n, 0:FULL * P], bank[0:PARTS, 0:FULL * P]).then_inc(emptied, 1)
                else:
                    for j in range(4):
                        step = (1 + j) * DH
                        to = kt[0:PARTS, s, j, FULL * P:FULL * P + 2 * step].rearrange("p (a c) -> p a c", a=2)[:, :, 0:DH]
                        src = bank[0:PARTS, j * DH:(j + 1) * DH].rearrange("p (o c) -> p o c", o=1).broadcast_to([PARTS, 2, DH])
                        ins = nc.scalar.copy(to, src)
                    ins.then_inc(emptied, 1)

            def empty_max(i, s, first):
                g = 2 * i + s
                if not first:
                    act.wait_ge(m_in[s], 16 * i)
                for n in range(2):
                    act.wait_ge(turned, TURNS * g + 5 + n + 1)
                    nc.scalar.copy(mrow[MAXROW:DEEP, s, n * HALF:(n + 1) * HALF], pmix[(5 + 32 + n) % 3][MAXROW:DEEP, :]).then_inc(emptied, 1)

            def exp(i, s, n, first):
                at = STEPS * (2 * i + s) + n
                act.wait_ge(s2_done, at + 1)
                if not (first and n < NE):
                    act.wait_ge(pv_done, at - NE + 1)
                nc.scalar.activation(e[:, n % NE if s == 0 else (n + STEPS) % NE], ps[n % 2][:], ACT.Exp, scale=SCALE).then_inc(exp_done, 1)

            def copy_sums(i, s, half, first=False):
                g = 2 * i + s
                act.wait_ge(pv_done, STEPS * g + PIECES * (half + 1))
                if half == 0 and not first:
                    act.wait_ge(att_stored[s], 16 * i)
                nc.scalar.copy(att[:, s, half * HALF:(half + 1) * HALF], pout[:]).then_inc(out_copied, 1)
                if not (isinstance(g, int) and g == 0 and half == 0):
                    act.wait_ge(sums_turned, 2 * g + half)
                nc.scalar.copy(sums[:], psum_e[half][:]).then_inc(sums_out, 1)

            def group(i, s, nxt, before=None, first=False):
                for n in range(STEPS):
                    exp(i, s, n, first)
                    if nxt and n < 5:
                        empty_k(*nxt, n, first)
                    if n == 0 and before:
                        copy_sums(*before, 1)
                    if n == PIECES:
                        copy_sums(i, s, 0, isinstance(i, int) and i == 0)
                    if nxt and n == MAX_AT + 1:
                        empty_max(*nxt, first)

            act.wait_ge(keyf_step, 4)
            for n in range(5):
                empty_k(0, 0, n, True)
            empty_max(0, 0, True)
            group(0, 0, (0, 1), None, True)
            group(0, 1, (1, 0), (0, 0))
            with act.Fori(1, GROUPS // 2 - 1) as i:
                group(i, 0, (i, 1), (i - 1, 1))
                group(i, 1, (i + 1, 0), (i, 0))
            last = GROUPS // 2 - 1
            group(last, 0, (last, 1), (last - 1, 1))
            group(last, 1, None, (last, 0))
            copy_sums(last, 1, 1)

        @block.tensor
        def _(pe):
            def turn_k(i, s, n, early=False):
                g = 2 * i + s
                if n == 0:
                    pe.wait_ge(gathered[s], 16 * PIECES * (i + 1))
                if not (early and n < 3):
                    pe.wait_ge(emptied, TURNS * g + n - 2)
                for c in range(FULL if n < 4 else 1):
                    last = nc.tensor.transpose(pmix[n % 3][0:PARTS, c * P:(c + 1) * P], rows[:, s, n * FULL + c, 0:PARTS], ident[:])
                last.then_inc(turned, 1)

            def turn_max(i, s):
                g = 2 * i + s
                pe.wait_ge(ma_done, g + 1)
                for n in range(2):
                    for c in range(4):
                        last = nc.tensor.transpose(pmix[(5 + 32 + n) % 3][0:DEEP, c * P:(c + 1) * P], ma[:, 4 * n + c], ident[:])
                    last.then_inc(turned, 1)

            def score_for_max(i, s, n0, n1):
                g = 2 * i + s
                for n in range(n0, n1):
                    if n == 0:
                        pe.wait_ge(q_in[s], 16 * 12 * (i + 1))
                        pe.wait_ge(emptied, TURNS * g + 5)
                    if n >= 3:
                        pe.wait_ge(s1_read, 32 * g + n - 2)
                    j, m = n // 8, n % 8
                    nc.tensor.matmul(pmix[(5 + n) % 3][:, 0:SLOTS], q[0:PARTS, s, j, m * P:(m + 1) * P], kt[0:PARTS, s, j, 0:SLOTS],
                                     start=True, stop=True).then_inc(s1_done, 1)

            def score(i, s, n, first=False):
                half, m = divmod(n, PIECES)
                at = STEPS * (2 * i + s) + n
                if n == 0:
                    pe.wait_ge(m_in[s], 16 * (i + 1))
                if not (first and n < 2):
                    pe.wait_ge(exp_done, at - 1)
                cols = slice(half * HALF, (half + 1) * HALF)
                if m < 4 * FULL:
                    c, j = divmod(m, 4)
                    last = nc.tensor.matmul(ps[n % 2][:], kt[0:DEEP, s, j, c * P:(c + 1) * P], q[0:DEEP, s, j, cols], start=True, stop=True)
                else:
                    for j in range(4):
                        last = nc.tensor.matmul(ps[n % 2][:], kt[0:DEEP, s, j, PAD:PAD + P], q[0:DEEP, s, j, cols], start=(j == 0), stop=(j == 3))
                last.then_inc(s2_done, 1)

            def head_rows(j):
                return slice(j * DH, (j + 1) * DH)

            def weigh(i, s, n, first=False):
                half, m = divmod(n, PIECES)
                g = 2 * i + s
                pe.wait_ge(exp_done, STEPS * g + n + 1)
                if m == 0 and not (first and half == 0):
                    pe.wait_ge(out_copied, 2 * g + half)
                if m == 0 and not first:
                    pe.wait_ge(att_done, 2 * g + half - 1)
                if n == 0:
                    pe.wait_ge(v_padded, 4 * g + 4)
                    pe.wait_ge(v_moved, g + 1)
                slot = n % NE if s == 0 else (n + STEPS) % NE
                if m < 4 * FULL:
                    c, j = divmod(m, 4)
                    at, other = head_rows(j), head_rows((j + 2) % 4)
                    nc.tensor.matmul(pout[at, :], v[:, s, j * FULL + c], e[:, slot], start=(c == 0), stop=False)
                    last = nc.tensor.matmul(psum_e[half][other, :], ones[:], e[:, slot], start=(c == 0), stop=False)
                else:
                    for j in range(4):
                        at, other = head_rows(j), head_rows((j + 2) % 4)
                        nc.tensor.matmul(pout[at, :], v_last[:, s, j], e[:, slot], start=False, stop=True)
                        last = nc.tensor.matmul(psum_e[half][other, :], ones_last[:, j], e[:, slot], start=False, stop=True)
                last.then_inc(pv_done, 1)

            def turn_sums(i, s, half):
                pe.wait_ge(sums_out, 2 * (2 * i + s) + half + 1)
                for c in range(HALF // P):
                    last = nc.tensor.matmul(psum_e[half][:, 4 * c:4 * c + 4], sums[:, c * P:(c + 1) * P], ident[:, 0:P:DH], start=True, stop=True)
                last.then_inc(sums_turned, 1)

            def spread_inverses(i, s, half):
                pe.wait_ge(inverted, 3 * (2 * (2 * i + s) + half) + 3)
                for c in range(HALF // P):
                    last = nc.tensor.transpose(psum_e[half][:, c * P:(c + 1) * P], wide[:, c * P:(c + 1) * P], ident[:])
                last.then_inc(spread, 1)

            def group(i, s, nxt, before=None, first=False):
                def next_scores(n0, n1):
                    if nxt:
                        score_for_max(*nxt, n0, min(n1, 32))

                for n in range(0, STEPS, 2):
                    done = max(0, 2 * n - 10)
                    for m in (n, n + 1):
                        if nxt and m < 5:
                            turn_k(*nxt, m)
                        elif n >= 6:
                            next_scores(done + m - n, done + m - n + 1)
                        score(i, s, m, first)
                    if n >= 6:
                        next_scores(done + 2, done + 3)
                    if n == PIECES - 1:
                        weighed = range(n - 2, n + 1)
                    elif n == PIECES + 1:
                        weighed = range(n - 1, n)
                    else:
                        weighed = range(max(n - 2, 0), n)
                    for m in weighed:
                        weigh(i, s, m, first)
                    if n == 4:
                        next_scores(0, 2)
                    elif n >= 6:
                        next_scores(done + 3, done + 4)
                    if before and n == 2:
                        turn_sums(*before, 1)
                    if before and n == 4:
                        spread_inverses(*before, 1)
                    if n == SUMS_AT:
                        turn_sums(i, s, 0)
                    if n == SUMS_AT + 2:
                        spread_inverses(i, s, 0)
                    if nxt and n == MAX_AT:
                        turn_max(*nxt)
                weigh(i, s, STEPS - 2, first)
                weigh(i, s, STEPS - 1, first)

            pe.wait_ge(consts, 64)
            pe.wait_ge(keyf_step, 4)
            pe.wait_ge(set_up, MEMSETS)
            for c in range(FULL):
                nc.tensor.transpose(pout[:, c * ROWS:(c + 1) * ROWS], keyf[:, c * P:(c + 1) * P], ident[0:ROWS, 0:ROWS])
            nc.tensor.transpose(pout[0:DH, FULL * ROWS:(FULL + 1) * ROWS], keyf[:, FULL * P:], ident[0:ROWS, 0:ROWS]).then_inc(key_turned, 1)
            for n in range(5):
                turn_k(0, 0, n, True)
            pe.wait_ge(indexed, FULL + 4)
            score_for_max(0, 0, 0, 32)
            turn_max(0, 0)
            group(0, 0, (0, 1), None, True)
            group(0, 1, (1, 0), (0, 0))
            with pe.Fori(1, GROUPS // 2 - 1) as i:
                group(i, 0, (i, 1), (i - 1, 1))
                group(i, 1, (i + 1, 0), (i, 0))
            last = GROUPS // 2 - 1
            group(last, 0, (last, 1), (last - 1, 1))
            group(last, 1, None, (last, 0))
            turn_sums(last, 1, 1)
            spread_inverses(last, 1, 1)


def project_out_and_route(nc, t):
    with ExitStack() as ctx:
        sb = lambda name, shape, dt=F32: ctx.enter_context(nc.sbuf_tensor(name, shape, dt))
        sem = lambda name: ctx.enter_context(nc.semaphore(name))
        psum = lambda name: ctx.enter_context(nc.psum_tensor(name, [P, 512], F32))
        w = sb("d_w", [P, KD, D])
        wh = sb("d_wh", [P, KD, D], F32R)
        wl = sb("d_wl", [P, KD, D], F32R)
        gate = sb("d_gate", [P, KD, EXPERTS])
        bias = sb("d_bias", [1, D])
        rest = sb("d_rest", [1, 2, D])
        part = sb("d_part", [1, 2, D], BF16)
        bias3 = sb("d_bias3", [P, D], BF16)
        ones = sb("d_ones", [P, P], BF16)
        ident = sb("d_ident", [P, P])
        eps = sb("d_eps", [P, 1])
        zero = sb("d_zero", [P, ROW])
        names = sb("d_names", [P, EXPERTS, CHOSEN])
        att = sb("d_att", [P, 2, KD, HALF])
        ah = sb("d_ah", [P, 2, KD, HALF], F32R)
        al = sb("d_al", [P, 2, KD, HALF], F32R)
        x = sb("d_x", [P, 2, 4, D])
        left = sb("d_left", [P, 2 * B, 4])
        xrow = sb("d_xrow", [P, 2, 4, D])
        gates = sb("d_gates", [P, 2, 4, EXPERTS])
        stats = sb("d_stats", [P, 4, 6])
        mv = sb("d_mv", [P, 4, 2])
        sd = sb("d_sd", [P, 4])
        rs = sb("d_rs", [P, 4])
        xt = sb("d_xt", [P, 2, KD, HALF])
        lt = sb("d_lt", [P, HALF])
        lg = sb("d_lg", [P, 4, EXPERTS])
        best = sb("d_best", [P, 4, 8])
        at = sb("d_at", [P, 4, 8], U32)
        nmax = sb("d_nmax", [P, 4])
        ex = sb("d_ex", [P, 4, EXPERTS])
        tot = sb("d_tot", [P, 4])
        itot = sb("d_itot", [P, 4])
        hit = sb("d_hit", [P, EXPERTS, CHOSEN])
        mask = sb("d_mask", [P, 4, EXPERTS])
        order = sb("d_order", [P, 4, EXPERTS])
        ordt = sb("d_ordt", [P, 2, HALF // 2])
        po = [psum(f"d_po{n}") for n in range(2)]
        pt = [psum(f"d_pt{n}") for n in range(2)]
        pg, pl, pk = psum("d_pg"), psum("d_pl"), psum("d_pk")
        consts, bias_in, zeroed, bias_step, rows_in = (sem(f"d_{n}") for n in ("consts", "bias_in", "zeroed", "bias_step", "rows_in"))
        wh_done, wl_done = sem("d_wh_done"), sem("d_wl_done")
        att_in = [sem(f"d_att_in{u}") for u in range(2)]
        x_in = [sem(f"d_x_in{u}") for u in range(2)]
        ah_done, al_done, projected, added, stat, aggregated = (sem(f"d_{n}") for n in ("ah_done", "al_done", "projected", "added", "stat", "aggregated"))
        rooted, inverted, normed, turned, xt_done = (sem(f"d_{n}") for n in ("rooted", "inverted", "normed", "turned", "xt_done"))
        gated, gate_out, lt_turned, ranked, nmax_done = (sem(f"d_{n}") for n in ("gated", "gate_out", "lt_turned", "ranked", "nmax_done"))
        exped, itot_done, masked, row_done, order_done = (sem(f"d_{n}") for n in ("exped", "itot_done", "masked", "row_done", "order_done"))
        order_turned, ordt_done, pad_stored = sem("d_order_turned"), sem("d_ordt_done"), sem("d_pad_stored")
        x1_stored = [sem(f"d_x1_stored{u}") for u in range(2)]
        row_stored = [sem(f"d_row_stored{u}") for u in range(2)]
        xt_stored = [sem(f"d_xt_stored{u}") for u in range(2)]
        gates_stored = [sem(f"d_gates_stored{u}") for u in range(2)]
        ord_stored = [sem(f"d_ord_stored{u}") for u in range(2)]
        block = ctx.enter_context(nc.Block())
        x_dram = t["x"].rearrange("b (u j p) d -> b u p j d", p=P, j=4)
        x1_dram = t["x1"].rearrange("(b u j p) d -> b u p j d", b=B, p=P, j=4)
        row_dram = t["xrow"][0:N].rearrange("(b u j p) d -> b u p j d", b=B, p=P, j=4)

        HALVES = 2 * B

        def before(b, u, d):
            return b + (u - d) // 2, (u - d) % 2

        def steps(engine, step):
            for u in range(2):
                step(0, u, u)
            with engine.Fori(1, B - 1) as b:
                for u in range(2):
                    step(b, u)
            for n in range(HALVES - 2, HALVES + 2):
                step(n // 2, n % 2, n)

        @block.sync
        def _(sp):
            sp.dma_start(w[:], t["wo"].rearrange("(k p) n -> p k n", p=P)).then_inc(consts, 16)
            sp.dma_start(gate[:], t["gate"].rearrange("(k p) n -> p k n", p=P)).then_inc(consts, 16)
            sp.dma_start(ident[:], t["ident"]).then_inc(consts, 16)
            sp.dma_start(names[:], t["expert_names"]).then_inc(consts, 16)
            sp.dma_start(bias[:], t["bo"].rearrange("(o n) -> o n", o=1)).then_inc(bias_in, 16)

            sp.dma_start(left[:], t["left"].rearrange("b u p j -> p (b u) j")).then_inc(consts, 16)

            def load_att(b, u):
                sp.dma_start(att[:, u], t["att"][b, :, :, u * HALF:(u + 1) * HALF].rearrange("g p s -> p g s")).then_inc(att_in[u], 16)

            def load_x(b, u):
                sp.dma_start(x[:, u], x_dram[b, u]).then_inc(x_in[u], 16)

            def step(b, u, late=None):
                n = 2 * b + u
                tiles = 4 * n if late is not None else sp.snap(4 * n)
                (b1, u1), (b2, u2) = before(b, u, 1), before(b, u, 2)
                if late is None or late + 2 < HALVES:
                    sp.wait_ge(al_done, n + 1)
                    load_att(b + 1, u)
                if late is None or 1 <= late <= HALVES:
                    sp.wait_ge(normed, tiles)
                    sp.dma_start(row_dram[b1, u1][:, :, 0:D], xrow[:, u1]).then_inc(row_stored[u1], 16)
                    sp.dma_start(x1_dram[b1, u1], x[:, u1]).then_inc(x1_stored[u1], 16)
                    if late is None or late + 1 < HALVES:
                        sp.wait_ge(x1_stored[u1], 16 * (b1 + 1))
                        load_x(b1 + 1, u1)
                    sp.wait_ge(xt_done, tiles)
                    sp.dma_start(t["xt2"][b1, u1], xt[:, u1]).then_inc(xt_stored[u1], 16)
                if late is None or late >= 2:
                    sp.wait_ge(row_done, tiles - 4)
                    sp.dma_start(row_dram[b2, u2][:, :, D:ROW], gates[:, u2]).then_inc(gates_stored[u2], 16)
                if late is None or late >= 2:
                    sp.wait_ge(ordt_done, n - 2 + 1)
                    for r in range(2):
                        sp.dma_start(t["order"][:, b2, u2].rearrange("e (j r p) -> r e j p", r=2, p=P)[r],
                                     ordt[r * EXPERTS:(r + 1) * EXPERTS, u2].rearrange("e (j p) -> e j p", p=P)).then_inc(ord_stored[u2], 16)

            load_att(0, 0)
            load_x(0, 0)
            load_att(0, 1)
            load_x(0, 1)
            sp.wait_ge(zeroed, 5)
            sp.dma_start(t["xrow"][N:N + P], zero[:]).then_inc(pad_stored, 16)
            steps(sp, step)
            sp.wait_ge(pad_stored, 16)
            for u in range(2):
                for stored in (x1_stored, row_stored, xt_stored, gates_stored):
                    sp.wait_ge(stored[u], 16 * B)
                sp.wait_ge(ord_stored[u], 32 * B)

        @block.vector
        def _(dve):
            nc.vector.memset(bias3[:], 0.0).then_inc(zeroed, 1)
            nc.vector.memset(ones[:], 1.0).then_inc(zeroed, 1)
            nc.vector.memset(zero[:], 0.0).then_inc(zeroed, 1)
            nc.vector.memset(eps[:], EPS).then_inc(zeroed, 1)
            nc.vector.memset(lt[:], 0.0).then_inc(zeroed, 1)
            dve.wait_ge(bias_in, 16)
            dve.wait_ge(zeroed, 2)
            nc.vector.tensor_copy(bias3[0:1, :], bias[:]).then_inc(bias_step, 1)
            dve.wait_ge(bias_step, 1)
            nc.vector.tensor_tensor(rest[:, 0], bias[:], bias3[0:1, :], ALU.subtract).then_inc(bias_step, 1)
            dve.wait_ge(bias_step, 2)
            nc.vector.tensor_copy(part[:, 0], rest[:, 0]).then_inc(bias_step, 1)
            dve.wait_ge(bias_step, 3)
            nc.vector.tensor_tensor(rest[:, 1], rest[:, 0], part[:, 0], ALU.subtract).then_inc(bias_step, 1)
            dve.wait_ge(bias_step, 4)
            nc.vector.tensor_copy(part[:, 1], rest[:, 1]).then_inc(bias_step, 1)
            for k in range(KD):
                dve.wait_ge(wh_done, k + 1)
                nc.vector.tensor_tensor(wl[:, k], w[:, k], wh[:, k].bitcast(F32), ALU.subtract).then_inc(wl_done, 1)
            dve.wait_ge(consts, 80)

            def split(b, u, n):
                dve.wait_ge(ah_done, n + 1)
                nc.vector.tensor_tensor(al[:, u], att[:, u], ah[:, u].bitcast(F32), ALU.subtract).then_inc(al_done, 1)

            def add(b, u, n, j):
                if j == 0:
                    dve.wait_ge(x_in[u], 16 * b + 16)
                dve.wait_ge(projected, 4 * n + j + 1)
                nc.vector.tensor_tensor(x[:, u, j], po[j % 2][:], x[:, u, j], ALU.add).then_inc(added, 1)
                dve.wait_ge(added, 4 * n + j + 1)
                nc.vector.bn_stats(stats[:, j], x[:, u, j]).then_inc(stat, 1)

            def normalise(b, u, n, first):
                dve.wait_ge(rooted, n + 1)
                nc.vector.reciprocal(rs[:], sd[:]).then_inc(inverted, 1)
                if not first:
                    dve.wait_ge(row_stored[u], 16 * b)
                dve.wait_ge(inverted, n + 1)
                for j in range(4):
                    nc.vector.tensor_scalar(xrow[:, u, j], x[:, u, j], mv[:, j, 0:1], rs[:, j:j + 1],
                                            ALU.subtract, ALU.mult).then_inc(normed, 1)

            def rank(b, u, n, first):
                dve.wait_ge(lt_turned, n + 1)
                if not first:
                    dve.wait_ge(row_done, 4 * n)
                    dve.wait_ge(order_turned, n)
                nc.vector.tensor_copy(lg[:], pl[:].rearrange("p (j e) -> p j e", j=4)[:, :, 0:EXPERTS]).then_inc(ranked, 1)
                dve.wait_ge(ranked, 1)
                for j in range(4):
                    nc.vector.max(best[:, j], lg[:, j]).then_inc(ranked, 1)
                for j in range(4):
                    dve.wait_ge(ranked, j + 2)
                    nc.vector.max_index(at[:, j], best[:, j], lg[:, j]).then_inc(ranked, 1)
                nc.vector.tensor_scalar(nmax[:], best[:, :, 0], -1.0, None, ALU.mult).then_inc(nmax_done, 1)
                for j in range(4):
                    dve.wait_ge(ranked, 9 + j)
                    nc.vector.tensor_tensor(hit[:], names[:], at[:, j, 0:CHOSEN].rearrange("p (o k) -> p o k", o=1).broadcast_to([P, EXPERTS, CHOSEN]),
                                            ALU.is_equal).then_inc(ranked, 1)
                    dve.wait_ge(ranked, 10 + j)
                    nc.vector.tensor_reduce(mask[:, j], hit[:], AX_X, ALU.add).then_inc(masked, 1)
                    dve.wait_ge(masked, 4 * n + j + 1)
                    nc.vector.tensor_scalar(order[:, j], mask[:, j], left[:, n, j:j + 1], None, ALU.mult).then_inc(order_done, 1)

            def gate_rows(b, u, n, first):
                dve.wait_ge(exped, 4 * n + 4)
                nc.vector.reciprocal(itot[:], tot[:]).then_inc(itot_done, 1)
                if not first:
                    dve.wait_ge(gates_stored[u], 16 * b)
                dve.wait_ge(itot_done, n + 1)
                for j in range(4):
                    nc.vector.scalar_tensor_tensor(out=gates[:, u, j], in0=ex[:, j], scalar=itot[:, j:j + 1], in1=mask[:, j],
                                                   op0=ALU.mult, op1=ALU.mult).then_inc(row_done, 1)

            def step(b, u, late=None):
                n = 2 * b + u
                here = late is None or late < HALVES
                before1, before2 = before(b, u, 1), before(b, u, 2)
                dve.sem_clear(stat)
                dve.sem_clear(ranked)
                if late is None or 1 <= late <= HALVES:
                    dve.wait_ge(aggregated, 4 * n)
                    normalise(*before1, n - 1, late in (1, 2))
                    dve.wait_ge(normed, 4 * n)
                if here:
                    add(b, u, n, 0)
                if late is None or late >= 2:
                    rank(*before2, n - 2, late == 2)
                if here:
                    add(b, u, n, 1)
                    add(b, u, n, 2)
                if late is None or late + 1 < HALVES:
                    split(b + (u + 1) // 2, 1 - u, n + 1)
                if late is None or late >= 2:
                    gate_rows(*before2, n - 2, late in (2, 3))
                if here:
                    add(b, u, n, 3)
                    for j in range(4):
                        dve.wait_ge(stat, j + 1)
                        nc.vector.bn_aggr(mv[:, j], stats[:, j]).then_inc(aggregated, 1)

            split(0, 0, 0)
            steps(dve, step)

        @block.scalar
        def _(act):
            act.wait_ge(consts, 80)
            for k in range(KD):
                nc.scalar.copy(wh[:, k], w[:, k]).then_inc(wh_done, 1)
            for r in range(2):
                act.wait_ge(bias_step, 3 + 2 * r)
                act.dma_start(bias3[1 + r:2 + r, :], part[:, r]).then_inc(rows_in, 16)
            act.wait_ge(zeroed, 5)

            def split(b, u, n, first):
                act.wait_ge(att_in[u], 16 * b + 16)
                if not first:
                    act.wait_ge(projected, 4 * (n - 1))
                nc.scalar.copy(ah[:, u], att[:, u]).then_inc(ah_done, 1)

            def step(b, u, late=None):
                n = 2 * b + u
                (b1, u1), (b2, u2) = before(b, u, 1), before(b, u, 2)
                if late is None or 1 <= late <= HALVES:
                    act.wait_ge(aggregated, 4 * (n - 1) + 4)
                    nc.scalar.activation(sd[:], mv[:, :, 1], ACT.Sqrt, bias=eps[:, 0:1]).then_inc(rooted, 1)
                    if late not in (1, 2):
                        act.wait_ge(xt_stored[u1], 16 * b1)
                    for k in range(KD):
                        act.wait_ge(turned, 4 * (n - 1) + k + 1)
                        nc.scalar.copy(xt[:, u1, k], pt[k % 2][:]).then_inc(xt_done, 1)
                if late is None or late >= 2:
                    act.wait_ge(nmax_done, n - 2 + 1)
                    for j in range(4):
                        nc.scalar.activation(ex[:, j], lg[:, j], ACT.Exp, bias=nmax[:, j:j + 1], accum_out=tot[:, j:j + 1]).then_inc(exped, 1)
                if late is None or late + 1 < HALVES:
                    split(b + (u + 1) // 2, 1 - u, n + 1, late == 0)
                if late is None or 1 <= late <= HALVES:
                    act.wait_ge(gated, n)
                    if late != 1:
                        act.wait_ge(lt_turned, n - 1)
                    nc.scalar.copy(lt[0:EXPERTS], pg[0:EXPERTS, :]).then_inc(gate_out, 1)
                if late is None or late >= 2:
                    act.wait_ge(order_turned, n - 2 + 1)
                    if late not in (2, 3):
                        act.wait_ge(ord_stored[u2], 32 * b2)
                    nc.scalar.copy(ordt[:, u2], pk[:, 0:HALF // 2]).then_inc(ordt_done, 1)

            split(0, 0, 0, True)
            steps(act, step)

        @block.tensor
        def _(pe):
            pe.wait_ge(consts, 80)
            pe.wait_ge(rows_in, 32)
            pe.wait_ge(bias_step, 1)
            pe.wait_ge(wl_done, KD)

            def project(u, n, j, first):
                if j == 0:
                    pe.wait_ge(al_done, n + 1)
                if not (first and j < 2):
                    pe.wait_ge(added, 4 * n + j - 1)
                rows = slice(j * P, (j + 1) * P)
                nc.tensor.matmul(po[j % 2][:], ones[:], bias3[:], start=True, stop=False)
                for k in range(KD):
                    nc.tensor.matmul(po[j % 2][:], ah[:, u, k, rows], wh[:, k], start=False, stop=False)
                    nc.tensor.matmul(po[j % 2][:], ah[:, u, k, rows], wl[:, k], start=False, stop=False)
                    last = nc.tensor.matmul(po[j % 2][:], al[:, u, k, rows], wh[:, k], start=False, stop=(k == KD - 1))
                last.then_inc(projected, 1)

            def step(b, u, late=None):
                n = 2 * b + u
                here = late is None or late < HALVES
                one = late is None or 1 <= late <= HALVES
                u1 = 1 - u
                if here:
                    project(u, n, 0, late == 0)
                    project(u, n, 1, late == 0)
                if one:
                    pe.wait_ge(normed, 4 * (n - 1) + 4)
                    for k in range(KD):
                        if not (late == 1 and k < 2):
                            pe.wait_ge(xt_done, 4 * (n - 1) + k - 1)
                        for j in range(4):
                            last = nc.tensor.transpose(pt[k % 2][:, j * P:(j + 1) * P], xrow[:, u1, j, k * P:(k + 1) * P], ident[:])
                        last.then_inc(turned, 1)
                if here:
                    project(u, n, 2, False)
                if one:
                    if late != 1:
                        pe.wait_ge(gate_out, n - 1)
                    for k in range(KD):
                        pe.wait_ge(xt_done, 4 * (n - 1) + k + 1)
                        last = nc.tensor.matmul(pg[0:EXPERTS, :], gate[:, k], xt[:, u1, k], start=(k == 0), stop=(k == KD - 1))
                    last.then_inc(gated, 1)
                if here:
                    project(u, n, 3, False)
                if late is None or late >= 2:
                    pe.wait_ge(order_done, 4 * (n - 2) + 4)
                    if late != 2:
                        pe.wait_ge(ordt_done, n - 2)
                    for j in range(2):
                        last = nc.tensor.transpose(pk[:, j * P:(j + 1) * P], order[:, 2 * j:2 * j + 2].rearrange("p j e -> p (j e)"), ident[:])
                    last.then_inc(order_turned, 1)
                if one:
                    if late != 1:
                        pe.wait_ge(nmax_done, n - 1)
                    pe.wait_ge(gate_out, n)
                    for j in range(4):
                        last = nc.tensor.transpose(pl[:, j * P:(j + 1) * P], lt[:, j * P:(j + 1) * P], ident[:])
                    last.then_inc(lt_turned, 1)

            steps(pe, step)


def shared_experts(nc, t):
    CH = SHARED_CHUNKS
    HALVES = 2 * B
    PIECES = 2
    PIECE = CH * D // PIECES
    with ExitStack() as ctx:
        sb = lambda name, shape, dt=F32: ctx.enter_context(nc.sbuf_tensor(name, shape, dt))
        sem = lambda name: ctx.enter_context(nc.semaphore(name))
        psum = lambda name: ctx.enter_context(nc.psum_tensor(name, [P, 512], F32))
        raw = sb("e_raw", [P, CH * D])
        up = {n: [sb(f"e_{n}{part}", [P, KD, CH * P], F32R) for part in "hl"] for n in ("sw1", "sw3")}
        down = [sb(f"e_sw2{part}", [P, CH, D], F32R) for part in "hl"]
        x = sb("e_x", [P, KD, HALF])
        xh = sb("e_xh", [P, 2, KD, HALF], F32R)
        xl = sb("e_xl", [P, 2, KD, HALF], F32R)
        silu = sb("e_silu", [P, 2, HALF])
        h = sb("e_h", [P, 2, HALF])
        hh = sb("e_hh", [P, 3, HALF], F32R)
        hl = sb("e_hl", [P, 3, HALF], F32R)
        shared = sb("e_shared", [P, 8, D])
        z, x1 = shared[:, 0:4], shared[:, 4:8]
        raw3 = shared[:, 0:CH].rearrange("p a b -> p (a b)")
        order = sb("e_order", [EXPERTS, N])
        top = sb("e_top", [EXPERTS, 8])
        first = sb("e_first", [EXPERTS, CAPACITY])
        p1 = [psum(f"e_p1{n}") for n in range(2)]
        p3 = [psum(f"e_p3{n}") for n in range(2)]
        pz = [psum(f"e_pz{n}") for n in range(4)]
        raw_in = [sem(f"e_raw_in{n}") for n in range(3)]
        split_h, split_l = sem("e_split_h"), sem("e_split_l")
        x_in, x1_in, xh_done, xl_done = sem("e_x_in"), sem("e_x1_in"), sem("e_xh_done"), sem("e_xl_done")
        up_done, silu_done, h_done, hh_done, hl_done, down_done = (
            sem(f"e_{n}") for n in ("up_done", "silu_done", "h_done", "hh_done", "hl_done", "down_done"))
        summed, stored = sem("e_summed"), sem("e_stored")
        order_in, ranked, list_stored = (sem(f"e_{n}") for n in ("order_in", "ranked", "list_stored"))
        block = ctx.enter_context(nc.Block())
        xt2 = t["xt2"].rearrange("b u p k s -> (b u) p k s")
        x1_dram = t["x1"].rearrange("(n j p) d -> n p j d", p=P, j=4)
        out_dram = t["out"][0:N].rearrange("(n j p) d -> n p j d", p=P, j=4)

        def flat(a):
            return a[:].rearrange("p a b -> p (a b)")

        weights = [("sw1", flat(up["sw1"][0]), flat(up["sw1"][1]), raw[:]), ("sw3", flat(up["sw3"][0]), flat(up["sw3"][1]), raw3),
                   ("sw2", flat(down[0]), flat(down[1]), raw[:])]

        def halves(engine, body):
            for u in range(2):
                body(u, u, u == 0, False)
            with engine.Fori(1, HALVES // 2 - 1) as i:
                for u in range(2):
                    body(2 * i + u, u, False, False)
            for u in range(2):
                body(HALVES - 2 + u, u, False, u == 1)

        @block.sync
        def _(sp):
            def load_weight(n):
                name, _, _, to = weights[n]
                k = CH if name == "sw2" else KD
                sp.dma_start(to.rearrange("p (k n) -> p k n", k=k), t[name].rearrange("(k p) n -> p k n", p=P)).then_inc(raw_in[n], 16)

            def finish(n):
                sp.wait_ge(summed, 4 * n + 4)
                sp.dma_start(out_dram[n], z).then_inc(stored, 16)

            def body(n, u, early, last):
                if not last:
                    sp.wait_ge(xl_done, KD * n + KD)
                    sp.dma_start(x[:], xt2[n + 1]).then_inc(x_in, 16)
                if not early:
                    finish(n - 1)
                    sp.dma_start(x1, x1_dram[n]).then_inc(x1_in, 16)

            load_weight(0)
            sp.dma_start(x[:], xt2[0]).then_inc(x_in, 16)
            load_weight(1)
            sp.wait_ge(split_l, PIECES)
            load_weight(2)
            sp.dma_start(order[:], t["order"].rearrange("e b u s -> e (b u s)")).then_inc(order_in, 16)
            sp.wait_ge(split_l, 2 * PIECES)
            sp.dma_start(x1, x1_dram[0]).then_inc(x1_in, 16)
            halves(sp, body)
            finish(HALVES - 1)
            sp.wait_ge(ranked, 3)
            sp.dma_start(t["first"], first[:]).then_inc(list_stored, 16)
            sp.wait_ge(stored, 16 * HALVES)
            sp.wait_ge(list_stored, 16)

        @block.vector
        def _(dve):
            def find(early):
                if early:
                    dve.wait_ge(order_in, 16)
                else:
                    dve.wait_ge(ranked, 3)
                dve.sem_clear(ranked)
                nc.vector.max(top[:], order[:]).then_inc(ranked, 1)

            def strike(r):
                dve.wait_ge(ranked, 1)
                nc.vector.match_replace(order[:], top[:], order[:], 0.0).then_inc(ranked, 1)
                nc.vector.tensor_copy(first[:, bass.ds(8 * r, 8)], top[:]).then_inc(ranked, 1)

            def add(n, early):
                dve.wait_ge(down_done, CH * n + CH)
                dve.wait_ge(x1_in, 16 * n + 16)
                if not early:
                    dve.wait_ge(stored, 16 * n)
                for j in range(4):
                    nc.vector.tensor_tensor(z[:, j], pz[j][:], x1[:, j], ALU.add).then_inc(summed, 1)

            def body(n, u, early, last):
                for m in range(CH):
                    at = CH * n + m
                    if m == 2 and not early:
                        add(n - 1, isinstance(n, int) and n == 1)
                    dve.wait_ge(silu_done, at + 1)
                    dve.wait_ge(up_done, 2 * at + 2)
                    if not (early and m < 2):
                        dve.wait_ge(hl_done, at - 1)
                    nc.vector.tensor_tensor(h[:, m % 2], silu[:, m % 2], p3[m % 2][:], ALU.mult).then_inc(h_done, 1)
                    if m in (0, 3):
                        find(early and m == 0)
                    elif m in (1, 4):
                        strike(2 * n + m // 3)

            for n, (name, high, low, src) in enumerate(weights):
                for c in range(PIECES):
                    at = slice(c * PIECE, (c + 1) * PIECE)
                    dve.wait_ge(split_h, PIECES * n + c + 1)
                    nc.vector.tensor_tensor(low[:, at], src[:, at], high[:, at].bitcast(F32), ALU.subtract).then_inc(split_l, 1)
            halves(dve, body)
            add(HALVES - 1, False)

        @block.scalar
        def _(act):
            def split(n, u, k):
                if k == 0:
                    act.wait_ge(x_in, 16 * n + 16)
                nc.scalar.copy(xh[:, u, k], x[:, k]).then_inc(xh_done, 1)

            def body(n, u, early, last):
                for m in range(CH):
                    at = CH * n + m
                    act.wait_ge(up_done, 2 * at + 1)
                    nc.scalar.activation(silu[:, m % 2], p1[m % 2][:], ACT.Silu).then_inc(silu_done, 1)
                    if m >= 1 and m <= KD and not last:
                        split(n + 1, 1 - u, m - 1)
                    act.wait_ge(h_done, at + 1)
                    if not (early and m < 3):
                        act.wait_ge(down_done, at - 2)
                    nc.scalar.copy(hh[:, m % 3], h[:, m % 2]).then_inc(hh_done, 1)

            for n, (name, high, low, src) in enumerate(weights):
                act.wait_ge(raw_in[n], 16)
                for c in range(PIECES):
                    at = slice(c * PIECE, (c + 1) * PIECE)
                    nc.scalar.copy(high[:, at], src[:, at]).then_inc(split_h, 1)
                if n == 0:
                    for k in range(KD):
                        split(0, 0, k)
            halves(act, body)

        @block.gpsimd
        def _(pool):
            def split(n, u, k):
                pool.wait_ge(xh_done, KD * n + k + 1)
                nc.gpsimd.tensor_tensor(xl[:, u, k], x[:, k], xh[:, u, k].bitcast(F32), ALU.subtract).then_inc(xl_done, 1)

            def body(n, u, early, last):
                for m in range(CH):
                    at = CH * n + m
                    if m >= 1 and m <= KD and not last:
                        split(n + 1, 1 - u, m - 1)
                    pool.wait_ge(hh_done, at + 1)
                    nc.gpsimd.tensor_tensor(hl[:, m % 3], h[:, m % 2], hh[:, m % 3].bitcast(F32), ALU.subtract).then_inc(hl_done, 1)

            for k in range(KD):
                split(0, 0, k)
            halves(pool, body)

        @block.tensor
        def _(pe):
            def rise(n, u, m, early):
                at = CH * n + m
                if m == 0:
                    pe.wait_ge(xl_done, KD * n + KD)
                if not (early and m < 2):
                    pe.wait_ge(h_done, at - 1)
                for r, (bank, name) in enumerate(((p1[m % 2], "sw1"), (p3[m % 2], "sw3"))):
                    if early and m == 0:
                        pe.wait_ge(split_l, PIECES * (r + 1))
                    high, low = up[name]
                    for k in range(KD):
                        cols = slice(m * P, (m + 1) * P)
                        nc.tensor.matmul(bank[:], high[:, k, cols], xh[:, u, k], start=(k == 0), stop=False)
                        nc.tensor.matmul(bank[:], high[:, k, cols], xl[:, u, k], start=False, stop=False)
                        last = nc.tensor.matmul(bank[:], low[:, k, cols], xh[:, u, k], start=False, stop=(k == KD - 1))
                    last.then_inc(up_done, 1)

            def fall(n, m, early):
                at = CH * n + m
                if early and m == 0:
                    pe.wait_ge(split_l, 3 * PIECES)
                pe.wait_ge(hl_done, at + 1)
                for j in range(4):
                    if m == 0 and not early:
                        pe.wait_ge(summed, 4 * n + j - 3)
                    rows = slice(j * P, (j + 1) * P)
                    nc.tensor.matmul(pz[j][:], hh[:, m % 3, rows], down[0][:, m], start=(m == 0), stop=False)
                    nc.tensor.matmul(pz[j][:], hh[:, m % 3, rows], down[1][:, m], start=False, stop=False)
                    last = nc.tensor.matmul(pz[j][:], hl[:, m % 3, rows], down[0][:, m], start=False, stop=(m == CH - 1))
                last.then_inc(down_done, 1)

            def body(n, u, early, last):
                for m in range(CH):
                    rise(n, u, m, early)
                    if m >= 2:
                        fall(n, m - 2, early)
                    elif not early:
                        fall(n - 1, CH - 2 + m, False)

            halves(pe, body)
            fall(HALVES - 1, CH - 2, False)
            fall(HALVES - 1, CH - 1, False)


def routed_experts(nc, t):
    TURN = 4
    CHUNKS = [(0, P), (P, P), (2 * P, INTER - 2 * P)]
    LAST = INTER - 2 * P
    TURNS = EXPERTS // TURN
    with ExitStack() as ctx:
        sb = lambda name, shape, dt=F32: ctx.enter_context(nc.sbuf_tensor(name, shape, dt))
        sem = lambda name: ctx.enter_context(nc.semaphore(name))
        psum = lambda name: ctx.enter_context(nc.psum_tensor(name, [P, 512], F32))
        w13 = sb("r_w13", [P, TURN, KD, 2 * INTER])
        w2 = sb("r_w2", [P, TURN, 3, D])
        ident = sb("r_ident", [P, P])
        slot = sb("r_slot", [P, 1])
        first = sb("r_first", [EXPERTS, CAPACITY])
        empty = sb("r_empty", [P, EXPERTS])
        row = sb("r_row", [P, EXPERTS])
        zero = sb("r_zero", [P, D])
        picked = sb("r_picked", [P, TURN], U32)
        added_to = sb("r_added_to", [P, TURN], U32)
        xe = sb("r_xe", [P, TURN, ROW])
        xt = sb("r_xt", [P, 2, KD * P])
        silu = sb("r_silu", [P, 2, 3 * P])
        h = sb("r_h", [P, 2, 3 * P])
        y = sb("r_y", [P, 2, D])
        p1 = [psum(f"r_p1{n}") for n in range(2)]
        p3 = [psum(f"r_p3{n}") for n in range(2)]
        pt = [psum(f"r_pt{n}") for n in range(2)]
        py = [psum(f"r_py{n}") for n in range(2)]
        consts, zero_set, zero_out, first_turned, rows_found = (sem(f"r_{n}") for n in ("consts", "zero_set", "zero_out", "first_turned", "rows_found"))
        w_in = [sem(f"r_w_in{s}") for s in range(TURN)]
        gathered = [sem(f"r_gathered{s}") for s in range(TURN)]
        picked_done = [sem(f"r_picked_done{s}") for s in range(TURN)]
        scaled = [sem(f"r_scaled{s}") for s in range(TURN)]
        turned, xt_done, up_done = (sem(f"r_{n}") for n in ("turned", "xt_done", "up_done"))
        silu_done, h_done, down_done, scattered, added = (sem(f"r_{n}") for n in ("silu_done", "h_done", "down_done", "scattered", "added"))
        block = ctx.enter_context(nc.Block())

        def turns(engine, body):
            body(0, 0)
            with engine.Fori(1, TURNS - 1) as i:
                body(i, None)
            body(TURNS - 1, EXPERTS - TURN)

        @block.sync
        def _(sp):
            sp.dma_start(first[:], t["first"]).then_inc(consts, 16)
            sp.dma_start(ident[:], t["ident"]).then_inc(consts, 16)
            sp.dma_start(slot[:], t["slot"]).then_inc(consts, 16)

            def load(i, s):
                e = TURN * i + s
                sp.dma_start(w13[:, s], t["w13"][e]).then_inc(w_in[s], 16)
                sp.dma_start(w2[:, s, 0:2], t["w2"][e, 0:2 * P].rearrange("(c p) d -> p c d", p=P)).then_inc(w_in[s], 16)
                sp.dma_start(w2[0:LAST, s, 2], t["w2"][e, 2 * P:INTER]).then_inc(w_in[s], 16)

            load(0, 0)
            sp.wait_ge(zero_set, 1)
            sp.dma_start(t["out"][N:N + P], zero[:]).then_inc(zero_out, 16)
            sp.wait_ge(gathered[0], 16)
            for s in range(1, TURN):
                load(0, s)
            with sp.Fori(1, TURNS) as i:
                for s in range(TURN):
                    sp.wait_ge(down_done, TURN * (i - 1) + s + 1)
                    load(i, s)
            sp.wait_ge(zero_out, 16)

        @block.gpsimd
        def _(pool):
            nc.gpsimd.memset(zero[:], 0.0).then_inc(zero_set, 1)

            def gather(e, s):
                pool.wait_ge(picked_done[s], 1)
                pool.sem_clear(picked_done[s])
                nc.gpsimd.indirect_dma_start(xe[:, s], None, t["xrow"], bass.IndirectOffsetOnAxis(picked[:, s:s + 1], 0)).then_inc(gathered[s], 16)

            def add_done(e):
                pool.wait_ge(scattered, 16 * (e + 1))
                pool.sem_inc(added, 1)

            def scatter(e, s, first):
                pool.wait_ge(scaled[s], 2)
                pool.sem_clear(scaled[s])
                if not first:
                    add_done(e - 1)
                nc.gpsimd.indirect_dma_start(t["out"], bass.IndirectOffsetOnAxis(added_to[:, s:s + 1], 0), y[:, s % 2], None, compute_op=ALU.add).then_inc(scattered, 16)

            def body(i, at):
                for s in range(TURN):
                    e = TURN * i + s
                    if at is None or at + s > 0:
                        scatter(e - 1, (s - 1) % TURN, at == 0 and s == 1)
                    if at is None or at + s + 3 < EXPERTS:
                        gather(e + 3, (s + 3) % TURN)

            for s in range(3):
                gather(s, s)
            pool.wait_ge(zero_out, 16)
            turns(pool, body)
            scatter(EXPERTS - 1, TURN - 1, False)
            add_done(EXPERTS - 1)

        @block.vector
        def _(dve):
            dve.wait_ge(first_turned, 1)
            nc.vector.tensor_scalar(empty[:], p1[0][:, 0:EXPERTS], 0.0, slot[:, 0:1], ALU.is_equal, ALU.mult).then_inc(rows_found, 1)
            nc.vector.tensor_scalar(row[:], p1[0][:, 0:EXPERTS], -1.0, float(N), ALU.mult, ALU.add).then_inc(rows_found, 1)
            dve.wait_ge(rows_found, 2)
            nc.vector.tensor_tensor(row[:], row[:], empty[:], ALU.add).then_inc(rows_found, 1)
            dve.wait_ge(rows_found, 3)

            def pick(e, s, i, first):
                if not first:
                    dve.wait_ge(gathered[s], 16 * i)
                nc.vector.tensor_scalar(picked[:, s:s + 1], row[:, bass.ds(e, 1)], 1.0, None, ALU.mult).then_inc(picked_done[s], 1)

            def multiply(e, s, first):
                b = s % 2
                dve.wait_ge(silu_done, 2 * e + 2)
                if not first:
                    dve.wait_ge(down_done, e - 1)
                nc.vector.tensor_tensor(h[:, b, 0:2 * P], silu[:, b, 0:2 * P], p3[b][:, 0:2 * P], ALU.mult).then_inc(h_done, 1)
                nc.vector.tensor_tensor(h[0:LAST, b, 2 * P:], silu[0:LAST, b, 2 * P:], p3[b][0:LAST, 2 * P:3 * P], ALU.mult).then_inc(h_done, 1)

            def scale(e, s, first):
                dve.wait_ge(down_done, e + 1)
                if not first:
                    dve.wait_ge(added, e - 1)
                nc.vector.tensor_scalar(added_to[:, s:s + 1], row[:, bass.ds(e, 1)], 1.0, None, ALU.mult).then_inc(scaled[s], 1)
                nc.vector.tensor_scalar(y[:, s % 2], py[s % 2][:], xe[:, s, bass.ds(e + D, 1)], None, ALU.mult).then_inc(scaled[s], 1)

            def body(i, at):
                for s in range(TURN):
                    e = TURN * i + s
                    multiply(e, s, at == 0 and s < 2)
                    if at is None or at + s > 0:
                        scale(e - 1, (s - 1) % TURN, at == 0 and s - 1 < 2)
                    if at is None or at + s + 3 < EXPERTS:
                        pick(e + 3, (s + 3) % TURN, i + (s + 3) // TURN, at == 0 and s == 0)

            for s in range(3):
                pick(s, s, 0, True)
            turns(dve, body)
            scale(EXPERTS - 1, TURN - 1, False)

        @block.scalar
        def _(act):
            def body(i, at):
                for s in range(TURN):
                    e = TURN * i + s
                    b = s % 2
                    act.wait_ge(up_done, e + 1)
                    if not (at == 0 and s < 2):
                        act.wait_ge(h_done, 2 * e - 2)
                    nc.scalar.activation(silu[:, b, 0:2 * P], p1[b][:, 0:2 * P], ACT.Silu).then_inc(silu_done, 1)
                    nc.scalar.activation(silu[0:LAST, b, 2 * P:], p1[b][0:LAST, 2 * P:3 * P], ACT.Silu).then_inc(silu_done, 1)
                    if at is None or at + s + 1 < EXPERTS:
                        act.wait_ge(turned, e + 2)
                        nc.scalar.copy(xt[:, 1 - b], pt[1 - b][:]).then_inc(xt_done, 1)

            act.wait_ge(turned, 1)
            nc.scalar.copy(xt[:, 0], pt[0][:]).then_inc(xt_done, 1)
            turns(act, body)

        @block.tensor
        def _(pe):
            pe.wait_ge(consts, 48)
            nc.tensor.transpose(p1[0][:, 0:EXPERTS], first[:], ident[0:EXPERTS, 0:EXPERTS]).then_inc(first_turned, 1)
            pe.wait_ge(rows_found, 2)

            def turn(e, s, i, first):
                pe.wait_ge(gathered[s], 16 * i + 16)
                if not first:
                    pe.wait_ge(xt_done, e - 1)
                for k in range(KD):
                    last = nc.tensor.transpose(pt[s % 2][:, k * P:(k + 1) * P], xe[:, s, k * P:(k + 1) * P], ident[:])
                last.then_inc(turned, 1)

            def rise(e, s, i, first):
                b = s % 2
                pe.wait_ge(xt_done, e + 1)
                pe.wait_ge(w_in[s], 48 * i + 48)
                if not first:
                    pe.wait_ge(h_done, 2 * e - 2)
                for bank, start in ((p1[b], 0), (p3[b], INTER)):
                    for c, (at, size) in enumerate(CHUNKS):
                        for k in range(KD):
                            last = nc.tensor.matmul(bank[0:size, c * P:(c + 1) * P], w13[:, s, k, start + at:start + at + size], xt[:, b, k * P:(k + 1) * P],
                                                    start=(k == 0), stop=(k == KD - 1))
                last.then_inc(up_done, 1)

            def fall(e, s, first):
                b = s % 2
                pe.wait_ge(h_done, 2 * e + 2)
                for c, (at, size) in enumerate(CHUNKS):
                    last = nc.tensor.matmul(py[b][:], h[0:size, b, c * P:(c + 1) * P], w2[0:size, s, c], start=(c == 0), stop=(c == 2))
                last.then_inc(down_done, 1)

            def body(i, at):
                for s in range(TURN):
                    e = TURN * i + s
                    rise(e, s, i, at == 0 and s < 2)
                    if at is None or at + s + 1 < EXPERTS:
                        turn(e + 1, (s + 1) % TURN, i + (s + 1) // TURN, at == 0 and s + 1 < 2)
                    if at is None or at + s > 0:
                        fall(e - 1, (s - 1) % TURN, at == 0 and s - 1 < 2)

            turn(0, 0, 0, True)
            turns(pe, body)
            fall(EXPERTS - 1, TURN - 1, False)


def clear_semaphores(nc, used):
    with nc.Block() as block:

        @block.vector
        def _(dve):
            for semaphore in used:
                dve.sem_clear(semaphore)


def decoder_layer_kernel(nc, t):
    for name, shape, dtype in (
        ("xnt", (2 * B, P, KD, HALF), F32),
        ("lg", (B, HEADS, S), F32),
        ("qh", (B, 4, S // P, P, P), F32),
        ("ql", (B, 4, S // P, P, P), F32),
        ("kv", (N * KV_HEADS, P), F32),
        ("keys", (B * HEADS, -(-TOPK // 8) * 8), U32),
        ("att", (B, 4, P, S), F32),
        ("x1", (N, D), F32),
        ("xrow", (N + P, ROW), F32),
        ("xt2", (B, 2, P, KD, HALF), F32),
        ("order", (EXPERTS, B, 2, HALF), F32),
        ("first", (EXPERTS, CAPACITY), F32),
    ):
        t[name] = nc.dram_tensor(f"{name}_scratch", shape, dtype).ap()
    clear_semaphores(nc, normalise_and_route(nc, t))
    project_and_rank(nc, t)
    attend(nc, t)
    project_out_and_route(nc, t)
    shared_experts(nc, t)
    routed_experts(nc, t)


def rotary_tables():
    import numpy as np

    pos = np.arange(S, dtype=np.float32)
    inv_freq = np.float32(1.0) / np.float32(1000000.0) ** (np.arange(0, DH, 2, dtype=np.float32) / np.float32(DH))
    freqs = pos[:, None] * inv_freq[None, :]
    cos, sin = np.cos(freqs), np.sin(freqs)
    both = np.stack([np.concatenate([cos, cos], -1), np.concatenate([sin, -sin], -1)], 1)
    return both.reshape(S // P, P, 2, DH).astype(np.float32)


def key_row_picks():
    import numpy as np

    full = TOPK // P * P
    padded = -(-TOPK // 8) * 8
    picks = np.zeros((DH, 4, 640), np.float32)
    for j in range(4):
        picks[2 * j:2 * j + 2, j, 0:full] = 1.0
        picks[2 * j:2 * j + 2, j, padded + DH * j:padded + DH * (j + 1)] = 1.0
    return picks


def kernel(**inputs):
    import numpy as np
    import concourse.bacc as _bacc
    from concourse import mybir as _mybir
    from concourse.bass_utils import run_bass_kernel_spmd as _run

    attn = lambda name: np.asarray(inputs[f"L0_attn_{name}"])
    ffn = lambda name: np.asarray(inputs[f"L0_ffn_{name}"])

    def chunked(w):
        return w.reshape(EXPERTS, INTER, KD, P).transpose(0, 3, 2, 1)

    wide = SHARED_CHUNKS * P - SHARED
    tokens = np.arange(N, dtype=np.float32)
    arrays = {
        "x": attn("hidden_states"),
        "wr": attn("Wr"), "br": attn("br"),
        "wq": attn("Wq"), "wk": attn("Wk"), "wv": attn("Wv"),
        "bq": attn("bq"), "bk": attn("bk"), "bv": attn("bv"),
        "wo": attn("Wo"), "bo": attn("bo"),
        "gate": ffn("gate_w").T,
        "sw1": np.pad(ffn("sw1").T, ((0, 0), (0, wide))),
        "sw3": np.pad(ffn("sw3").T, ((0, 0), (0, wide))),
        "sw2": np.pad(ffn("sw2").T, ((0, wide), (0, 0))),
        "w13": np.concatenate([chunked(ffn("w1")), chunked(ffn("w3"))], -1),
        "w2": ffn("w2").transpose(0, 2, 1),
        "ident": np.eye(P, dtype=np.float32),
        "cs": rotary_tables(),
        "kv_base": np.array([[b * S * KV_HEADS + h * KV_HEADS // HEADS] for b in range(B) for h in range(HEADS)], np.float32),
        "pick_rows": key_row_picks(),
        "expert_names": np.broadcast_to(np.arange(EXPERTS, dtype=np.float32)[None, :, None], (P, EXPERTS, CHOSEN)),
        "left": (N - tokens).reshape(B, 2, HALF // P, P).transpose(0, 1, 3, 2),
        "slot": np.arange(CAPACITY, dtype=np.float32)[:, None],
    }
    arrays = {name: np.ascontiguousarray(a) for name, a in arrays.items()}
    nc = _bacc.Bacc("TRN2", target_bir_lowering=False, num_devices=1)
    t = {name: nc.dram_tensor(name, a.shape, _mybir.dt.from_np(a.dtype), kind="ExternalInput").ap() for name, a in arrays.items()}
    t["out"] = nc.dram_tensor("out", (N + P, D), _mybir.dt.float32, kind="ExternalOutput").ap()
    decoder_layer_kernel(nc, t)
    got = _run(nc, [arrays], core_ids=[0])
    return got.results[0]["out"][:N].reshape(B, S, D)
```

```python
import math
from contextlib import ExitStack

import concourse.bass as bass
import concourse.mybir as mybir
from concourse.alu_op_type import AluOpType as ALU

ACT = mybir.ActivationFunctionType
F32, F32R, BF16, U32 = mybir.dt.float32, mybir.dt.float32r, mybir.dt.bfloat16, mybir.dt.uint32
AX_X = mybir.AxisListType.X

P = 128
B, S, D = 4, 1024, 512
N = B * S
HEADS, KV_HEADS, DH = 16, 8, 32
KD = D // P
HALF = 512
TILES = N // P
TOPK = int(S * 0.4)
EPS = 1e-5
EXPERTS, CHOSEN, CAPACITY, INTER = 64, 6, 128, 352
ROW = D + EXPERTS
SHARED = 704
SHARED_CHUNKS = -(-SHARED // P)


class Projection:

    def __init__(self, nc, ctx, name, columns):
        self.nc, self.columns = nc, columns
        self.high = ctx.enter_context(nc.sbuf_tensor(f"{name}_high", [P, KD, columns], F32R))
        self.low = ctx.enter_context(nc.sbuf_tensor(f"{name}_low", [P, KD, columns], F32R))
        self.bias = ctx.enter_context(nc.sbuf_tensor(f"{name}_bias", [P, columns], BF16))
        self.ones = ctx.enter_context(nc.sbuf_tensor(f"{name}_ones", [P, P], BF16))

    def open(self, ctx, name, sem):
        sb = lambda part, shape, dt=F32: ctx.enter_context(self.nc.sbuf_tensor(f"{name}_{part}", shape, dt))
        self.raw = sb("raw", [P, KD, self.columns])
        self.whole = sb("whole", [1, self.columns])
        self.rest = sb("rest", [1, 2, self.columns])
        self.part = sb("part", [1, 2, self.columns], BF16)
        self.raw_in, self.whole_in, self.zeroed = sem(f"{name}_raw_in"), sem(f"{name}_whole_in"), sem(f"{name}_zeroed")
        self.step, self.rows_in = sem(f"{name}_step"), sem(f"{name}_rows_in")
        self.high_done, self.low_done = sem(f"{name}_high_done"), sem(f"{name}_low_done")

    def load(self, sp, weights, biases):
        at = 0
        for weight, bias in zip(weights, biases):
            cols = slice(at, at + weight.shape[1])
            sp.dma_start(self.raw[:, :, cols], weight.rearrange("(k p) n -> p k n", p=P)).then_inc(self.raw_in, 16)
            sp.dma_start(self.whole[:, cols], bias.rearrange("(o n) -> o n", o=1)).then_inc(self.whole_in, 16)
            at += weight.shape[1]
        self.loads = len(weights)

    def take_high(self, act, k):
        if k == 0:
            act.wait_ge(self.raw_in, 16 * self.loads)
        self.nc.scalar.copy(self.high[:, k], self.raw[:, k]).then_inc(self.high_done, 1)

    def place_rows(self, act):
        for r in range(2):
            act.wait_ge(self.step, 3 + 2 * r)
            act.dma_start(self.bias[1 + r:2 + r, :], self.part[:, r]).then_inc(self.rows_in, 16)

    def take_low(self, dve, k):
        dve.wait_ge(self.high_done, k + 1)
        self.nc.vector.tensor_tensor(self.low[:, k], self.raw[:, k], self.high[:, k].bitcast(F32), ALU.subtract).then_inc(self.low_done, 1)

    def zero(self):
        self.nc.vector.memset(self.bias[:], 0.0).then_inc(self.zeroed, 1)
        self.nc.vector.memset(self.ones[:], 1.0).then_inc(self.zeroed, 1)

    def split_bias(self, dve, n):
        vector, rest, part = self.nc.vector, self.rest, self.part
        if n == 0:
            dve.wait_ge(self.whole_in, 16 * self.loads)
            dve.wait_ge(self.zeroed, 2)
            vector.tensor_copy(self.bias[0:1, :], self.whole[:]).then_inc(self.step, 1)
            return
        dve.wait_ge(self.step, n)
        if n == 1:
            vector.tensor_tensor(rest[:, 0], self.whole[:], self.bias[0:1, :], ALU.subtract).then_inc(self.step, 1)
        elif n == 2:
            vector.tensor_copy(part[:, 0], rest[:, 0]).then_inc(self.step, 1)
        elif n == 3:
            vector.tensor_tensor(rest[:, 1], rest[:, 0], part[:, 0], ALU.subtract).then_inc(self.step, 1)
        else:
            vector.tensor_copy(part[:, 1], rest[:, 1]).then_inc(self.step, 1)


def normalise_and_route(nc, t, qkv):
    HALVES, SLOTS = 2 * B, 4
    with ExitStack() as ctx:
        sb = lambda name, shape, dt=F32: ctx.enter_context(nc.sbuf_tensor(name, shape, dt))
        used = []

        def sem(name):
            used.append(ctx.enter_context(nc.semaphore(name)))
            return used[-1]

        x = sb("a_x", [P, SLOTS, 4, D])
        xt = sb("a_xt", [P, 2, KD, HALF])
        stats = sb("a_stats", [P, 2, 4, 6])
        mv = sb("a_mv", [P, 2, 4, 2])
        sd = sb("a_sd", [P, 2, 4])
        rs = sb("a_rs", [P, 2, 4])
        eps = sb("a_eps", [P, 1])
        wr = sb("a_wr", [P, KD, HEADS])
        br = sb("a_br", [HEADS, 1])
        ident = sb("a_ident", [P, P])
        lg = sb("a_lg", [HEADS, 2, HALF])
        turned = [ctx.enter_context(nc.psum_tensor(f"a_turned{k}", [P, HALF], F32)) for k in range(KD)]
        logits = [ctx.enter_context(nc.psum_tensor(f"a_logits{u}", [P, HALF], F32)) for u in range(2)]
        consts = sem("a_consts")
        x_in = [sem(f"a_x_in{s}") for s in range(SLOTS)]
        eps_set = sem("a_eps_set")
        stat_step = sem("a_stat_step")
        aggregated = sem("a_aggregated")
        rooted = sem("a_rooted")
        inverted = sem("a_inverted")
        normed = sem("a_normed")
        turned_done = sem("a_turned_done")
        evacuated = sem("a_evacuated")
        logits_done = sem("a_logits_done")
        logits_out = sem("a_logits_out")
        xt_stored = [sem(f"a_xt_stored{u}") for u in range(2)]
        lg_stored = [sem(f"a_lg_stored{u}") for u in range(2)]
        qkv.open(ctx, "a_qkv", sem)
        block = ctx.enter_context(nc.Block())

        x_dram = t["x"].rearrange("b (u j p) d -> (b u) p j d", p=P, j=4)

        @block.sync
        def _(sp):
            for n in range(HALVES):
                if n >= SLOTS:
                    sp.wait_ge(turned_done, KD * (n - SLOTS + 1))
                sp.dma_start(x[:, n % SLOTS], x_dram[n]).then_inc(x_in[n % SLOTS], 16)
                if n == 0:
                    sp.dma_start(ident[:], t["ident"]).then_inc(consts, 16)
                    sp.dma_start(wr[:], t["wr"].rearrange("(k p) h -> p k h", p=P)).then_inc(consts, 16)
                    sp.dma_start(br[:], t["br"].rearrange("(h o) -> h o", o=1)).then_inc(consts, 16)
                if n == SLOTS - 1:
                    qkv.load(sp, [t["wq"], t["wk"], t["wv"]], [t["bq"], t["bk"], t["bv"]])

        @block.vector
        def _(dve):
            def take_stats(n):
                u = n % 2
                dve.wait_ge(x_in[n % SLOTS], 16 * (n // SLOTS + 1))
                for j in range(4):
                    nc.vector.bn_stats(stats[:, u, j], x[:, n % SLOTS, j]).then_inc(stat_step, 1)
                for j in range(4):
                    dve.wait_ge(stat_step, 4 * n + j + 1)
                    nc.vector.bn_aggr(mv[:, u, j], stats[:, u, j]).then_inc(aggregated, 1)

            nc.vector.memset(eps[:], EPS).then_inc(eps_set, 1)
            qkv.zero()
            take_stats(0)
            for n in range(HALVES):
                u = n % 2
                if n + 1 < HALVES:
                    if n >= 1:
                        dve.wait_ge(normed, 4 * n)
                        dve.wait_ge(aggregated, 4 * n)
                    take_stats(n + 1)
                dve.wait_ge(rooted, n + 1)
                nc.vector.reciprocal(rs[:, u], sd[:, u]).then_inc(inverted, 1)
                dve.wait_ge(inverted, n + 1)
                for j in range(4):
                    rows = x[:, n % SLOTS, j]
                    nc.vector.tensor_scalar(rows, rows, mv[:, u, j, 0:1], rs[:, u, j:j + 1], ALU.subtract, ALU.mult).then_inc(normed, 1)
                if n >= 3:
                    qkv.split_bias(dve, n - 3)
                if n >= 4:
                    qkv.take_low(dve, n - 4)

        @block.scalar
        def _(act):
            def root(n):
                act.wait_ge(aggregated, 4 * n + 4)
                if n >= 2:
                    act.wait_ge(inverted, n - 1)
                nc.scalar.activation(sd[:, n % 2], mv[:, n % 2, :, 1], ACT.Sqrt, bias=eps[:, 0:1]).then_inc(rooted, 1)

            def finish(n):
                u = n % 2
                act.wait_ge(logits_done, n + 1)
                if n >= 2:
                    act.wait_ge(lg_stored[u], 16 * (n // 2))
                nc.scalar.activation(lg[:, u], logits[u][0:HEADS, :], ACT.Identity, bias=br[:, 0:1]).then_inc(logits_out, 1)
                act.wait_ge(logits_out, n + 1)
                act.dma_start(t["lg"][n // 2, :, u * HALF:(u + 1) * HALF], lg[:, u]).then_inc(lg_stored[u], 16)

            act.wait_ge(eps_set, 1)
            root(0)
            root(1)
            act.wait_ge(consts, 48)
            for n in range(HALVES):
                u = n % 2
                if n >= 2:
                    act.wait_ge(xt_stored[u], 16 * (n // 2))
                for k in range(KD):
                    act.wait_ge(turned_done, KD * n + k + 1)
                    nc.scalar.copy(xt[:, u, k], turned[k][:]).then_inc(evacuated, 1)
                act.wait_ge(evacuated, KD * n + KD)
                act.dma_start(t["xnt"][n], xt[:, u]).then_inc(xt_stored[u], 16)
                if 2 <= n < 2 + KD:
                    qkv.take_high(act, n - 2)
                if n + 2 < HALVES:
                    root(n + 2)
                if n:
                    finish(n - 1)
            qkv.place_rows(act)
            finish(HALVES - 1)
            act.wait_ge(qkv.rows_in, 32)
            for u in range(2):
                act.wait_ge(xt_stored[u], 16 * B)
                act.wait_ge(lg_stored[u], 16 * B)

        @block.tensor
        def _(pe):
            pe.wait_ge(consts, 48)

            def turn(n):
                pe.wait_ge(normed, 4 * n + 4)
                for k in range(KD):
                    if n:
                        pe.wait_ge(evacuated, KD * (n - 1) + k + 1)
                    for j in range(4):
                        last = nc.tensor.transpose(turned[k][:, j * P:(j + 1) * P], x[:, n % SLOTS, j, k * P:(k + 1) * P], ident[:])
                    last.then_inc(turned_done, 1)

            def route(n):
                if n >= 2:
                    pe.wait_ge(logits_out, n - 1)
                for k in range(KD):
                    pe.wait_ge(evacuated, KD * n + k + 1)
                    last = nc.tensor.matmul(logits[n % 2][0:HEADS, :], wr[:, k], xt[:, n % 2, k], start=(k == 0), stop=(k == KD - 1))
                last.then_inc(logits_done, 1)

            turn(0)
            for n in range(HALVES):
                if n + 1 < HALVES:
                    turn(n + 1)
                route(n)
    return used


def project_and_rank(nc, t, qkv):
    QK = (HEADS + KV_HEADS) * DH
    ROWS = B * HEADS
    ROUNDS = -(-TOPK // 8)
    with ExitStack() as ctx:
        sb = lambda name, shape, dt=F32: ctx.enter_context(nc.sbuf_tensor(name, shape, dt))
        sem = lambda name: ctx.enter_context(nc.semaphore(name))
        wh, wl, bias3, ones = qkv.high, qkv.low, qkv.bias, qkv.ones
        ident = sb("b_ident", [P, P])
        x = sb("b_x", [P, 2, KD, P])
        xh = sb("b_xh", [P, 2, KD, P], F32R)
        xl = sb("b_xl", [P, 2, KD, P], F32R)
        cs = sb("b_cs", [P, 2, 2, DH])
        qk = sb("b_qk", [P, 2, QK])
        qkc = sb("b_qkc", [P, QK])
        qks = sb("b_qks", [P, QK])
        rot = sb("b_rot", [P, 2, QK])
        kvrow = sb("b_kvrow", [P, 2, KV_HEADS, 4 * DH])
        qt = sb("b_qt", [P, 2, HEADS * DH])
        qh = sb("b_qh", [P, 2, HEADS * DH], F32R)
        ql = sb("b_ql", [P, 2, HEADS * DH], F32R)
        lg = sb("b_lg", [ROWS, S])
        top = sb("b_top", [ROWS, 8])
        at = sb("b_at", [ROWS, 8], U32)
        keys = sb("b_keys", [ROWS, ROUNDS * 8], U32)
        psum = lambda name: ctx.enter_context(nc.psum_tensor(name, [P, 512], F32))
        pq = [psum(f"b_pq{u}") for u in range(2)]
        pkv = [psum(f"b_pkv{u}") for u in range(2)]
        pt = [psum(f"b_pt{u}") for u in range(2)]
        lg_in, ident_in = sem("b_lg_in"), sem("b_ident_in")
        x_in = [sem(f"b_x_in{u}") for u in range(2)]
        cs_in = [sem(f"b_cs_in{u}") for u in range(2)]
        xh_done, xl_done = sem("b_xh_done"), sem("b_xl_done")
        projected, copied, v_copied = sem("b_projected"), sem("b_copied"), sem("b_v_copied")
        multiplied, rotated = sem("b_multiplied"), sem("b_rotated")
        turned, qt_done, kh_done = sem("b_turned"), sem("b_qt_done"), sem("b_kh_done")
        ql_done, kl_done = sem("b_ql_done"), sem("b_kl_done")
        q_stored = [sem(f"b_q_stored{u}") for u in range(2)]
        kv_stored = [sem(f"b_kv_stored{u}") for u in range(2)]
        ranked, kept, keys_stored = sem("b_ranked"), sem("b_kept"), sem("b_keys_stored")
        block = ctx.enter_context(nc.Block())
        xnt = t["xnt"].rearrange("a p k (j c) -> a j p k c", c=P)
        kv = t["kv"].rearrange("(n p h) c -> n p h c", p=P, h=KV_HEADS)

        def tile(i, u):
            return i // 4, 2 * (i % 4) + u

        @block.sync
        def _(sp):
            def load_x(i, u):
                sp.dma_start(x[:, u], xnt[i // 2, 2 * (i % 2) + u]).then_inc(x_in[u], 16)

            def load_cs(i, u):
                sp.dma_start(cs[:, u], t["cs"][tile(i, u)[1]]).then_inc(cs_in[u], 16)

            def store(i, u):
                b, j = tile(i, u)
                sp.wait_ge(ql_done, 2 * i + u + 1)
                for name, src in (("qh", qh), ("ql", ql)):
                    sp.dma_start(t[name][b, :, j].rearrange("g p c -> p g c"),
                                 src[:, u].bitcast(F32).rearrange("p (g c) -> p g c", c=P)).then_inc(q_stored[u], 16)
                sp.wait_ge(kl_done, 2 * i + u + 1)
                sp.wait_ge(v_copied, 2 * i + u + 1)
                sp.dma_start(kv[2 * i + u], kvrow[:, u]).then_inc(kv_stored[u], 16)

            def step(i, last=0):
                if last != 1:
                    sp.wait_ge(xl_done, 2 * i + 2)
                    load_x(i + 1, 1)
                    sp.wait_ge(multiplied, 4 * i + 2)
                    load_cs(i + 1, 0)
                if not (isinstance(i, int) and i == 0):
                    store(i - 1, 1)
                if not last:
                    sp.wait_ge(xl_done, 2 * i + 3)
                    load_x(i + 2, 0)
                if last != 1:
                    sp.wait_ge(multiplied, 4 * i + 4)
                    load_cs(i + 1, 1)
                store(i, 0)

            for u in range(2):
                load_x(0, u)
                load_cs(0, u)
            sp.dma_start(ident[:], t["ident"]).then_inc(ident_in, 16)
            sp.dma_start(lg[:], t["lg"].rearrange("b h s -> (b h) s")).then_inc(lg_in, 16)
            sp.wait_ge(xl_done, 1)
            load_x(1, 0)
            step(0)
            with sp.Fori(1, TILES // 2 - 2) as i:
                step(i)
            step(TILES // 2 - 2, last=2)
            step(TILES // 2 - 1, last=1)
            store(TILES // 2 - 1, 1)
            sp.wait_ge(kept, 1)
            sp.dma_start(t["keys"], keys[:]).then_inc(keys_stored, 16)
            for u in range(2):
                sp.wait_ge(q_stored[u], 32 * (TILES // 2))
                sp.wait_ge(kv_stored[u], 16 * (TILES // 2))
            sp.wait_ge(keys_stored, 16)

        @block.vector
        def _(dve):

            def rank(r):
                dve.sem_clear(ranked)
                nc.vector.max(top[:], lg[:]).then_inc(ranked, 1)
                dve.wait_ge(ranked, 1)
                nc.vector.max_index(at[:], top[:], lg[:]).then_inc(ranked, 1)
                dve.wait_ge(ranked, 2)
                nc.vector.match_replace(lg[:], top[:], lg[:], -3e38).then_inc(ranked, 1)
                nc.vector.tensor_copy(keys[:, bass.ds(8 * r, 8)], at[:]).then_inc(ranked, 1)
                dve.wait_ge(ranked, 4)

            def split(i, u, first=False):
                dve.wait_ge(xh_done, 2 * i + u + 1)
                if not first:
                    dve.wait_ge(projected, 4 * i + 2 * u - 2)
                nc.vector.tensor_tensor(xl[:, u], x[:, u], xh[:, u].bitcast(F32), ALU.subtract).then_inc(xl_done, 1)

            def step(i, r=None):
                for u in range(2):
                    split(i + 1, u)
                    if r is not None:
                        rank(r + 2 * u)
                        rank(r + 2 * u + 1)

            split(0, 0, True)
            split(0, 1, True)
            dve.wait_ge(lg_in, 16)
            with dve.Fori(0, ROUNDS // 4) as i:
                step(i, 4 * i)
            for i in range(ROUNDS // 4, TILES // 2 - 1):
                step(i)
            nc.vector.tensor_copy(keys[:, TOPK:], keys[:, TOPK - 1:TOPK].broadcast_to([ROWS, ROUNDS * 8 - TOPK])).then_inc(kept, 1)

        @block.scalar
        def _(act):
            def split(i, u, first=False):
                act.wait_ge(x_in[u], 16 * i + 16)
                if not first:
                    act.wait_ge(projected, 4 * i + 2 * u - 2)
                nc.scalar.copy(xh[:, u], x[:, u]).then_inc(xh_done, 1)

            def copy_out(i, u, first=False):
                act.wait_ge(projected, 4 * i + 2 * u + 1)
                if not first:
                    act.wait_ge(multiplied, 4 * i + 2 * u - 2)
                nc.scalar.copy(qk[:, u, 0:D], pq[u][:]).then_inc(copied, 1)
                act.wait_ge(projected, 4 * i + 2 * u + 2)
                nc.scalar.copy(qk[:, u, D:QK], pkv[u][:, 0:D // 2]).then_inc(copied, 1)
                if not first:
                    act.wait_ge(kv_stored[u], 16 * i)
                nc.scalar.copy(kvrow[:, u, :, 3 * DH:], pkv[u][:, D // 2:].rearrange("p (h c) -> p h c", c=DH)).then_inc(v_copied, 1)

            def finish(i, u, first=False):
                act.wait_ge(turned, 2 * i + u + 1)
                if not first:
                    act.wait_ge(q_stored[u], 32 * i)
                nc.scalar.copy(qt[:, u], pt[u][:]).then_inc(qt_done, 1)
                nc.scalar.copy(qh[:, u], pt[u][:]).then_inc(qt_done, 1)
                act.wait_ge(rotated, 4 * i + 2 * u + 2)
                k = rot[:, u, D:QK].rearrange("p (h o c) -> p h o c", o=1, c=DH)
                nc.scalar.copy(kvrow[:, u, :, 0:2 * DH].rearrange("p h (o c) -> p h o c", c=DH).bitcast(F32R),
                               k.broadcast_to([P, KV_HEADS, 2, DH])).then_inc(kh_done, 1)

            split(0, 0, True)
            split(0, 1, True)
            copy_out(0, 0, True)
            split(1, 0)
            copy_out(0, 1, True)
            finish(0, 0, True)
            split(1, 1)
            copy_out(1, 0)
            finish(0, 1, True)
            with act.Fori(1, TILES // 2 - 1) as i:
                split(i + 1, 0)
                copy_out(i, 1)
                finish(i, 0)
                split(i + 1, 1)
                copy_out(i + 1, 0)
                finish(i, 1)
            last = TILES // 2 - 1
            copy_out(last, 1)
            finish(last, 0)
            finish(last, 1)

        @block.gpsimd
        def _(pool):
            def rotate(i, u, first=False, second=False):
                pool.wait_ge(copied, 4 * i + 2 * u + 2)
                pool.wait_ge(cs_in[u], 16 * i + 16)
                if not first:
                    pool.wait_ge(rotated, 4 * i + 2 * u)
                heads = lambda a: a.rearrange("p (h c) -> p h c", c=DH)
                src = heads(qk[:, u])
                table = lambda n: cs[:, u, n:n + 1, :].broadcast_to([P, HEADS + KV_HEADS, DH])
                nc.gpsimd.tensor_tensor(heads(qkc[:]), src, table(0), ALU.mult).then_inc(multiplied, 1)
                nc.gpsimd.tensor_tensor(heads(qks[:]), src, table(1), ALU.mult).then_inc(multiplied, 1)
                pool.wait_ge(multiplied, 4 * i + 2 * u + 2)
                if not (first or second):
                    pool.wait_ge(turned, 2 * i + u - 1)
                    pool.wait_ge(kl_done, 2 * i + u - 1)
                for a, b in ((0, DH // 2), (DH // 2, 0)):
                    nc.gpsimd.tensor_tensor(heads(rot[:, u])[:, :, a:a + DH // 2], heads(qkc[:])[:, :, a:a + DH // 2],
                                            heads(qks[:])[:, :, b:b + DH // 2], ALU.add).then_inc(rotated, 1)

            def finish(i, u):
                pool.wait_ge(qt_done, 4 * i + 2 * u + 2)
                nc.gpsimd.tensor_tensor(ql[:, u], qt[:, u], qh[:, u].bitcast(F32), ALU.subtract).then_inc(ql_done, 1)
                pool.wait_ge(kh_done, 2 * i + u + 1)
                nc.gpsimd.tensor_tensor(kvrow[:, u, :, 2 * DH:3 * DH].bitcast(F32R), rot[:, u, D:QK].rearrange("p (h c) -> p h c", c=DH),
                                        kvrow[:, u, :, 0:DH], ALU.subtract).then_inc(kl_done, 1)

            rotate(0, 0, first=True)
            rotate(0, 1, second=True)
            finish(0, 0)
            rotate(1, 0)
            finish(0, 1)
            with pool.Fori(1, TILES // 2 - 1) as i:
                rotate(i, 1)
                finish(i, 0)
                rotate(i + 1, 0)
                finish(i, 1)
            last = TILES // 2 - 1
            rotate(last, 1)
            finish(last, 0)
            finish(last, 1)

        @block.tensor
        def _(pe):
            def project(i, u, first=False):
                pe.wait_ge(xl_done, 2 * i + u + 1)
                for n, out in enumerate((pq[u], pkv[u])):
                    if not first:
                        if n == 0:
                            pe.wait_ge(copied, 4 * i + 2 * u - 3)
                        else:
                            pe.wait_ge(v_copied, 2 * i + u - 1)
                    cols = slice(n * D, (n + 1) * D)
                    nc.tensor.matmul(out[:], ones[:], bias3[:, cols], start=True, stop=False)
                    for k in range(KD):
                        nc.tensor.matmul(out[:], xh[:, u, k], wh[:, k, cols], start=False, stop=False)
                        nc.tensor.matmul(out[:], xh[:, u, k], wl[:, k, cols], start=False, stop=False)
                        last = nc.tensor.matmul(out[:], xl[:, u, k], wh[:, k, cols], start=False, stop=(k == KD - 1))
                    last.then_inc(projected, 1)

            def turn(i, u, first=False):
                pe.wait_ge(rotated, 4 * i + 2 * u + 2)
                if not first:
                    pe.wait_ge(qt_done, 4 * i + 2 * u - 2)
                for g in range(4):
                    last = nc.tensor.transpose(pt[u][:, g * P:(g + 1) * P], rot[:, u, g * P:(g + 1) * P], ident[:])
                last.then_inc(turned, 1)

            pe.wait_ge(ident_in, 16)
            project(0, 0, True)
            project(0, 1, True)
            turn(0, 0, True)
            project(1, 0)
            turn(0, 1, True)
            with pe.Fori(1, TILES // 2 - 1) as i:
                project(i, 1)
                turn(i, 0)
                project(i + 1, 0)
                turn(i, 1)
            last = TILES // 2 - 1
            project(last, 1)
            turn(last, 0)
            turn(last, 1)


def attend(nc, t, wo):
    ROWS = B * HEADS
    SLOTS = -(-TOPK // 8) * 8
    FULL = TOPK // P
    LAST = TOPK - FULL * P
    PIECES = 4 * FULL + 1
    GROUPS = ROWS // 4
    PARTS = 3 * DH
    MAXROW = PARTS
    MAX_AT, SUMS_AT = 22, 14
    DEEP = MAXROW + 8
    PAD = SLOTS
    KTW = 640
    TURNS = 7
    STEPS = 2 * PIECES
    NE = 4
    SCALE = 1.0 / math.sqrt(DH)
    with ExitStack() as ctx:
        sb = lambda name, shape, dt=F32: ctx.enter_context(nc.sbuf_tensor(name, shape, dt))
        sem = lambda name: ctx.enter_context(nc.semaphore(name))
        psum = lambda name: ctx.enter_context(nc.psum_tensor(name, [P, 512], F32))
        ident = sb("c_ident", [P, P])
        keyu = sb("c_keyu", [ROWS, SLOTS], U32)
        keyf = sb("c_keyf", [ROWS, SLOTS])
        base = sb("c_base", [ROWS, 1])
        rowidx = sb("c_rowidx", [P, GROUPS, PIECES], U32)
        picked = sb("c_picked", [P, 2, PIECES], U32)
        rows = sb("c_rows", [P, 2, PIECES, P])
        pick_rows = sb("c_pick_rows", [P, 4, KTW])
        kt = sb("c_kt", [P, 2, 4, KTW], F32R)
        q = sb("c_q", [P, 2, 4, S], F32R)
        mx = sb("c_mx", [P, 8, 4])
        neg = sb("c_neg", [P, 8, 4])
        ma = sb("c_ma", [P, 8, DEEP])
        mrow = sb("c_mrow", [P, 2, S], F32R)
        e = sb("c_e", [P, NE, HALF])
        ones = sb("c_ones", [P, DH])
        ones_last = sb("c_ones_last", [P, 4, DH])
        v = sb("c_v", [P, 2, PIECES - 1, DH])
        v_last = sb("c_v_last", [P, 2, 4, DH])
        sums = sb("c_sums", [P, HALF])
        inv = sb("c_inv", [P, 4 * HALF // P])
        wide = sb("c_wide", [P, HALF])
        att = sb("c_att", [P, 2, S])
        ps = [psum(f"c_ps{n}") for n in range(2)]
        pmix = [psum(f"c_pmix{n}") for n in range(3)]
        pout = psum("c_pout")
        psum_e = [psum(f"c_psum{n}") for n in range(2)]
        consts, set_up, keyf_step, key_turned, indexed = (sem(f"c_{n}") for n in ("consts", "set_up", "keyf_step", "key_turned", "indexed"))
        key_in, picked_done = sem("c_key_in"), sem("c_picked_done")
        gathered = [sem(f"c_gathered{s}") for s in range(2)]
        q_in = [sem(f"c_q_in{s}") for s in range(2)]
        m_in = [sem(f"c_m_in{s}") for s in range(2)]
        v_padded, v_moved, turned, emptied = sem("c_v_padded"), sem("c_v_moved"), sem("c_turned"), sem("c_emptied")
        s1_done, s1_read, negated, ma_done = sem("c_s1_done"), sem("c_s1_read"), sem("c_negated"), sem("c_ma_done")
        s2_done, exp_done, pv_done, att_done = (sem(f"c_{n}") for n in ("s2_done", "exp_done", "pv_done", "att_done"))
        sums_out, out_copied, sums_turned, inverted, spread = (sem(f"c_{n}") for n in ("sums_out", "out_copied", "sums_turned", "inverted", "spread"))
        att_stored = [sem(f"c_att_stored{s}") for s in range(2)]
        wo.open(ctx, "c_wo", sem)
        block = ctx.enter_context(nc.Block())
        q_dram = {n: t[n].rearrange("b g j p c -> (b g) j p c") for n in ("qh", "ql")}
        att_dram = t["att"].rearrange("b g p s -> (b g) p s")
        MEMSETS = 5 + 4

        @block.sync
        def _(sp):
            sp.dma_start(keyu[:], t["keys"]).then_inc(key_in, 16)
            sp.dma_start(base[:], t["kv_base"]).then_inc(key_in, 16)
            sp.dma_start(ident[:], t["ident"]).then_inc(consts, 16)
            sp.dma_start(pick_rows[MAXROW:P], t["pick_rows"]).then_inc(consts, 16)

            def load_q(i, s):
                for j in range(4):
                    for part, name in enumerate(("qh", "ql", "qh")):
                        sp.dma_start(q[part * DH:(part + 1) * DH, s, j].bitcast(F32).rearrange("p (t c) -> p t c", c=P),
                                     q_dram[name][2 * i + s, :, j * DH:(j + 1) * DH].rearrange("t p c -> p t c")).then_inc(q_in[s], 16)

            def load_max(i, s):
                sp.wait_ge(emptied, TURNS * (2 * i + s) + TURNS)
                sp.dma_start(q[MAXROW:DEEP, s].bitcast(F32),
                             mrow[MAXROW:DEEP, s].bitcast(F32).rearrange("p (o c) -> p o c", o=1).broadcast_to([DEEP - MAXROW, 4, S])).then_inc(m_in[s], 16)

            def store(i, s):
                sp.wait_ge(att_done, 4 * i + 2 * s + 2)
                sp.dma_start(att_dram[2 * i + s], att[:, s]).then_inc(att_stored[s], 16)

            load_q(0, 0)
            load_q(0, 1)
            wo.load(sp, [t["wo"]], [t["bo"]])
            load_max(0, 0)
            with sp.Fori(0, GROUPS // 2 - 1) as i:
                load_max(i, 1)
                sp.wait_ge(s2_done, STEPS * (2 * i + 1))
                load_q(i + 1, 0)
                store(i, 0)
                load_max(i + 1, 0)
                sp.wait_ge(s2_done, STEPS * (2 * i + 2))
                load_q(i + 1, 1)
                store(i, 1)
            last = GROUPS // 2 - 1
            load_max(last, 1)
            store(last, 0)
            store(last, 1)
            for s in range(2):
                sp.wait_ge(att_stored[s], 16 * (GROUPS // 2))

        @block.gpsimd
        def _(pool):
            nc.gpsimd.memset(kt[:].bitcast(F32), 0.0).then_inc(set_up, 1)
            nc.gpsimd.memset(ma[:], 0.0).then_inc(set_up, 1)
            nc.gpsimd.memset(ones[:], 1.0).then_inc(set_up, 1)
            nc.gpsimd.memset(ones_last[:], 0.0).then_inc(set_up, 1)
            nc.gpsimd.memset(v_last[:], 0.0).then_inc(set_up, 1)
            pool.wait_ge(set_up, 5)
            for j in range(4):
                nc.gpsimd.memset(ones_last[j * DH:j * DH + LAST, j], 1.0).then_inc(set_up, 1)
            pool.wait_ge(set_up, MEMSETS)
            pool.wait_ge(indexed, FULL + 4)

            def gather(i, s, waits=True):
                pool.sem_clear(picked_done)
                if waits:
                    pool.wait_ge(turned, TURNS * (2 * i + s - 2) + 5)
                    pool.wait_ge(v_moved, 2 * i + s - 1)
                group = pool.snap(2 * i + s)
                nc.gpsimd.tensor_copy(picked[:, s], rowidx[:, group]).then_inc(picked_done, 1)
                pool.wait_ge(picked_done, 1)
                for n in range(PIECES):
                    nc.gpsimd.indirect_dma_start(rows[:, s, n], None, t["kv"], bass.IndirectOffsetOnAxis(picked[:, s, n:n + 1], 0)).then_inc(gathered[s], 16)

            gather(0, 0, False)
            gather(0, 1, False)
            with pool.Fori(1, GROUPS // 2) as i:
                gather(i, 0)
                gather(i, 1)

        TURN_AT = 2 * SUMS_AT - 6
        SPREAD_AT = TURN_AT + 4

        @block.vector
        def _(dve):
            dve.wait_ge(key_in, 32)
            nc.vector.tensor_copy(keyf[:], keyu[:]).then_inc(keyf_step, 1)
            dve.wait_ge(keyf_step, 1)
            nc.vector.tensor_scalar(keyf[:], keyf[:], float(KV_HEADS), base[:, 0:1], ALU.mult, ALU.add).then_inc(keyf_step, 1)
            dve.wait_ge(key_turned, 1)
            for c in range(FULL):
                nc.vector.tensor_copy(rowidx[:, :, c:4 * FULL:FULL], pout[:, c * ROWS:(c + 1) * ROWS].rearrange("p (g j) -> p g j", j=4)).then_inc(indexed, 1)
            for j in range(4):
                nc.vector.tensor_copy(rowidx[j * DH:(j + 1) * DH, :, PIECES - 1],
                                      pout[0:DH, FULL * ROWS:(FULL + 1) * ROWS].rearrange("p (g j) -> p g j", j=4)[:, :, j]).then_inc(indexed, 1)

            def move_v(i, s):
                dve.wait_ge(gathered[s], 16 * PIECES * (i + 1))
                nc.vector.tensor_copy(v[:, s], rows[:, s, 0:PIECES - 1, PARTS:]).then_inc(v_padded, 1)
                for j in range(4):
                    nc.vector.tensor_copy(v_last[j * DH:j * DH + LAST, s, j], rows[j * DH:j * DH + LAST, s, PIECES - 1, PARTS:]).then_inc(v_moved if j == 3 else v_padded, 1)

            def maxima(i, s, n0, n1):
                for n in range(n0, n1):
                    dve.wait_ge(s1_done, 32 * (2 * i + s) + n + 1)
                    nc.vector.tensor_reduce(mx[:, n % 8, n // 8:n // 8 + 1], pmix[(5 + n) % 3][:, 0:SLOTS], AX_X, ALU.max).then_inc(s1_read, 1)

            def negate(i, s, first=False):
                g = 2 * i + s
                dve.wait_ge(s1_read, 32 * g + 32)
                nc.vector.tensor_scalar(neg[:], mx[:], -1.0, None, ALU.mult).then_inc(negated, 1)
                dve.wait_ge(negated, 2 * g + 1)
                if not first:
                    dve.wait_ge(turned, TURNS * g)
                nc.vector.tensor_copy(ma[:, :, MAXROW:DEEP:2].bitcast(F32R), neg[:]).then_inc(negated, 1)
                dve.wait_ge(negated, 2 * g + 2)
                nc.vector.tensor_tensor(ma[:, :, MAXROW + 1:DEEP:2], neg[:], ma[:, :, MAXROW:DEEP:2], ALU.subtract).then_inc(ma_done, 1)

            def invert(i, s, half):
                g = 2 * i + s
                dve.wait_ge(sums_turned, 2 * g + half + 1)
                nc.vector.reciprocal(inv[:], psum_e[half][:, 0:4 * HALF // P]).then_inc(inverted, 1)
                dve.wait_ge(inverted, 3 * (2 * g + half) + 1)
                for k in range(2):
                    here, there = slice(2 * k, 2 * k + 2), slice(2 - 2 * k, 4 - 2 * k)
                    nc.vector.tensor_copy(wide[:].rearrange("p (c j o) -> p c j o", j=4, o=DH)[:, :, here],
                                          inv[:].rearrange("p (c j o) -> p c j o", j=4, o=1)[:, :, there].broadcast_to([P, HALF // P, 2, DH])).then_inc(inverted, 1)

            def normalise(i, s, half):
                g = 2 * i + s
                dve.wait_ge(out_copied, 2 * g + half + 1)
                dve.wait_ge(spread, 2 * g + half + 1)
                rows = att[:, s, half * HALF:(half + 1) * HALF]
                nc.vector.tensor_tensor(rows, rows, psum_e[half][:], ALU.mult).then_inc(att_done, 1)

            def copy_sums(i, s):
                g = 2 * i + s
                dve.wait_ge(pv_done, STEPS * g + STEPS)
                dve.wait_ge(sums_turned, 2 * g + 1)
                nc.vector.tensor_copy(sums[:], psum_e[1][:]).then_inc(sums_out, 1)

            def group(i, s, nxt, before):
                if before:
                    copy_sums(*before)
                    invert(*before, 1)
                if nxt:
                    move_v(*nxt)
                    maxima(*nxt, 0, 2)
                if before:
                    normalise(*before, 1)
                if nxt:
                    maxima(*nxt, 2, TURN_AT)
                invert(i, s, 0)
                if nxt:
                    maxima(*nxt, TURN_AT, SPREAD_AT)
                normalise(i, s, 0)
                if nxt:
                    maxima(*nxt, SPREAD_AT, 32)
                    negate(*nxt)

            dve.wait_ge(consts, 32)
            dve.wait_ge(set_up, MEMSETS)
            for s in range(2):
                nc.vector.tensor_copy(kt[MAXROW:P, s], pick_rows[MAXROW:P]).then_inc(keyf_step, 1)
            wo.zero()
            for n in range(5):
                wo.split_bias(dve, n)
            for k in range(KD):
                wo.take_low(dve, k)
            move_v(0, 0)
            maxima(0, 0, 0, 32)
            negate(0, 0, True)
            group(0, 0, (0, 1), None)
            group(0, 1, (1, 0), (0, 0))
            with dve.Fori(1, GROUPS // 2 - 1) as i:
                group(i, 0, (i, 1), (i - 1, 1))
                group(i, 1, (i + 1, 0), (i, 0))
            last = GROUPS // 2 - 1
            group(last, 0, (last, 1), (last - 1, 1))
            group(last, 1, None, (last, 0))
            copy_sums(last, 1)
            invert(last, 1, 1)
            normalise(last, 1, 1)

        @block.scalar
        def _(act):
            def empty_k(i, s, n, first=False):
                g = 2 * i + s
                if n == 0 and not first:
                    act.wait_ge(s2_done, STEPS * (g - 1))
                act.wait_ge(turned, TURNS * g + n + 1)
                bank = pmix[n % 3]
                if n < 4:
                    nc.scalar.copy(kt[0:PARTS, s, n, 0:FULL * P], bank[0:PARTS, 0:FULL * P]).then_inc(emptied, 1)
                else:
                    for j in range(4):
                        step = (1 + j) * DH
                        to = kt[0:PARTS, s, j, FULL * P:FULL * P + 2 * step].rearrange("p (a c) -> p a c", a=2)[:, :, 0:DH]
                        src = bank[0:PARTS, j * DH:(j + 1) * DH].rearrange("p (o c) -> p o c", o=1).broadcast_to([PARTS, 2, DH])
                        ins = nc.scalar.copy(to, src)
                    ins.then_inc(emptied, 1)

            def empty_max(i, s, first):
                g = 2 * i + s
                if not first:
                    act.wait_ge(m_in[s], 16 * i)
                for n in range(2):
                    act.wait_ge(turned, TURNS * g + 5 + n + 1)
                    nc.scalar.copy(mrow[MAXROW:DEEP, s, n * HALF:(n + 1) * HALF], pmix[(5 + 32 + n) % 3][MAXROW:DEEP, :]).then_inc(emptied, 1)

            def exp(i, s, n, first):
                at = STEPS * (2 * i + s) + n
                act.wait_ge(s2_done, at + 1)
                if not (first and n < NE):
                    act.wait_ge(pv_done, at - NE + 1)
                nc.scalar.activation(e[:, n % NE if s == 0 else (n + STEPS) % NE], ps[n % 2][:], ACT.Exp, scale=SCALE).then_inc(exp_done, 1)

            def copy_sums(i, s, half, first=False):
                g = 2 * i + s
                act.wait_ge(pv_done, STEPS * g + PIECES * (half + 1))
                if half == 0 and not first:
                    act.wait_ge(att_stored[s], 16 * i)
                nc.scalar.copy(att[:, s, half * HALF:(half + 1) * HALF], pout[:]).then_inc(out_copied, 1)
                if half == 0:
                    if not (isinstance(g, int) and g == 0):
                        act.wait_ge(sums_turned, 2 * g)
                    nc.scalar.copy(sums[:], psum_e[half][:]).then_inc(sums_out, 1)

            def group(i, s, nxt, before=None, first=False):
                for n in range(STEPS):
                    exp(i, s, n, first)
                    if nxt and n < 5:
                        empty_k(*nxt, n, first)
                    if n == 0 and before:
                        copy_sums(*before, 1)
                    if n == PIECES:
                        copy_sums(i, s, 0, isinstance(i, int) and i == 0)
                    if nxt and n == MAX_AT + 1:
                        empty_max(*nxt, first)

            for k in range(KD):
                wo.take_high(act, k)
            wo.place_rows(act)
            act.wait_ge(keyf_step, 4)
            for n in range(5):
                empty_k(0, 0, n, True)
            empty_max(0, 0, True)
            group(0, 0, (0, 1), None, True)
            group(0, 1, (1, 0), (0, 0))
            with act.Fori(1, GROUPS // 2 - 1) as i:
                group(i, 0, (i, 1), (i - 1, 1))
                group(i, 1, (i + 1, 0), (i, 0))
            last = GROUPS // 2 - 1
            group(last, 0, (last, 1), (last - 1, 1))
            group(last, 1, None, (last, 0))
            copy_sums(last, 1, 1)
            act.wait_ge(wo.rows_in, 32)

        @block.tensor
        def _(pe):
            def turn_k(i, s, n, early=False):
                g = 2 * i + s
                if n == 0:
                    pe.wait_ge(gathered[s], 16 * PIECES * (i + 1))
                if not (early and n < 3):
                    pe.wait_ge(emptied, TURNS * g + n - 2)
                for c in range(FULL if n < 4 else 1):
                    last = nc.tensor.transpose(pmix[n % 3][0:PARTS, c * P:(c + 1) * P], rows[:, s, n * FULL + c, 0:PARTS], ident[:])
                last.then_inc(turned, 1)

            def turn_max(i, s):
                g = 2 * i + s
                pe.wait_ge(ma_done, g + 1)
                for n in range(2):
                    for c in range(4):
                        last = nc.tensor.transpose(pmix[(5 + 32 + n) % 3][0:DEEP, c * P:(c + 1) * P], ma[:, 4 * n + c], ident[:])
                    last.then_inc(turned, 1)

            def score_for_max(i, s, n0, n1):
                g = 2 * i + s
                for n in range(n0, n1):
                    if n == 0:
                        pe.wait_ge(q_in[s], 16 * 12 * (i + 1))
                        pe.wait_ge(emptied, TURNS * g + 5)
                    if n >= 3:
                        pe.wait_ge(s1_read, 32 * g + n - 2)
                    j, m = n // 8, n % 8
                    nc.tensor.matmul(pmix[(5 + n) % 3][:, 0:SLOTS], q[0:PARTS, s, j, m * P:(m + 1) * P], kt[0:PARTS, s, j, 0:SLOTS],
                                     start=True, stop=True).then_inc(s1_done, 1)

            def score(i, s, n, first=False):
                half, m = divmod(n, PIECES)
                at = STEPS * (2 * i + s) + n
                if n == 0:
                    pe.wait_ge(m_in[s], 16 * (i + 1))
                if not (first and n < 2):
                    pe.wait_ge(exp_done, at - 1)
                cols = slice(half * HALF, (half + 1) * HALF)
                if m < 4 * FULL:
                    c, j = divmod(m, 4)
                    last = nc.tensor.matmul(ps[n % 2][:], kt[0:DEEP, s, j, c * P:(c + 1) * P], q[0:DEEP, s, j, cols], start=True, stop=True)
                else:
                    for j in range(4):
                        last = nc.tensor.matmul(ps[n % 2][:], kt[0:DEEP, s, j, PAD:PAD + P], q[0:DEEP, s, j, cols], start=(j == 0), stop=(j == 3))
                last.then_inc(s2_done, 1)

            def head_rows(j):
                return slice(j * DH, (j + 1) * DH)

            def weigh(i, s, n, first=False):
                half, m = divmod(n, PIECES)
                g = 2 * i + s
                pe.wait_ge(exp_done, STEPS * g + n + 1)
                if m == 0 and not (first and half == 0):
                    pe.wait_ge(out_copied, 2 * g + half)
                if m == 0 and not first:
                    pe.wait_ge(att_done, 2 * g + half - 1)
                if n == 0:
                    pe.wait_ge(v_padded, 4 * g + 4)
                    pe.wait_ge(v_moved, g + 1)
                slot = n % NE if s == 0 else (n + STEPS) % NE
                if m < 4 * FULL:
                    c, j = divmod(m, 4)
                    at, other = head_rows(j), head_rows((j + 2) % 4)
                    nc.tensor.matmul(pout[at, :], v[:, s, j * FULL + c], e[:, slot], start=(c == 0), stop=False)
                    last = nc.tensor.matmul(psum_e[half][other, :], ones[:], e[:, slot], start=(c == 0), stop=False)
                else:
                    for j in range(4):
                        at, other = head_rows(j), head_rows((j + 2) % 4)
                        nc.tensor.matmul(pout[at, :], v_last[:, s, j], e[:, slot], start=False, stop=True)
                        last = nc.tensor.matmul(psum_e[half][other, :], ones_last[:, j], e[:, slot], start=False, stop=True)
                last.then_inc(pv_done, 1)

            def turn_sums(i, s, half):
                pe.wait_ge(sums_out, 2 * (2 * i + s) + half + 1)
                for c in range(HALF // P):
                    last = nc.tensor.matmul(psum_e[half][:, 4 * c:4 * c + 4], sums[:, c * P:(c + 1) * P], ident[:, 0:P:DH], start=True, stop=True)
                last.then_inc(sums_turned, 1)

            def spread_inverses(i, s, half):
                pe.wait_ge(inverted, 3 * (2 * (2 * i + s) + half) + 3)
                for c in range(HALF // P):
                    last = nc.tensor.transpose(psum_e[half][:, c * P:(c + 1) * P], wide[:, c * P:(c + 1) * P], ident[:])
                last.then_inc(spread, 1)

            def group(i, s, nxt, before=None, first=False):
                def next_scores(n0, n1):
                    if nxt:
                        score_for_max(*nxt, n0, min(n1, 32))

                for n in range(0, STEPS, 2):
                    done = max(0, 2 * n - 10)
                    for m in (n, n + 1):
                        if nxt and m < 5:
                            turn_k(*nxt, m)
                        elif n >= 6:
                            next_scores(done + m - n, done + m - n + 1)
                        score(i, s, m, first)
                    if n >= 6:
                        next_scores(done + 2, done + 3)
                    if n == PIECES - 1:
                        weighed = range(n - 2, n + 1)
                    elif n == PIECES + 1:
                        weighed = range(n - 1, n)
                    else:
                        weighed = range(max(n - 2, 0), n)
                    for m in weighed:
                        weigh(i, s, m, first)
                    if n == 4:
                        next_scores(0, 2)
                    elif n >= 6:
                        next_scores(done + 3, done + 4)
                    if before and n == 2:
                        turn_sums(*before, 1)
                    if before and n == 4:
                        spread_inverses(*before, 1)
                    if n == SUMS_AT:
                        turn_sums(i, s, 0)
                    if n == SUMS_AT + 2:
                        spread_inverses(i, s, 0)
                    if nxt and n == MAX_AT:
                        turn_max(*nxt)
                weigh(i, s, STEPS - 2, first)
                weigh(i, s, STEPS - 1, first)

            pe.wait_ge(consts, 32)
            pe.wait_ge(keyf_step, 2)
            for c in range(FULL):
                nc.tensor.transpose(pout[:, c * ROWS:(c + 1) * ROWS], keyf[:, c * P:(c + 1) * P], ident[0:ROWS, 0:ROWS])
            nc.tensor.transpose(pout[0:DH, FULL * ROWS:(FULL + 1) * ROWS], keyf[:, FULL * P:], ident[0:ROWS, 0:ROWS]).then_inc(key_turned, 1)
            for n in range(5):
                turn_k(0, 0, n, True)
            pe.wait_ge(keyf_step, 4)
            pe.wait_ge(set_up, MEMSETS)
            pe.wait_ge(indexed, FULL + 4)
            score_for_max(0, 0, 0, 32)
            turn_max(0, 0)
            group(0, 0, (0, 1), None, True)
            group(0, 1, (1, 0), (0, 0))
            with pe.Fori(1, GROUPS // 2 - 1) as i:
                group(i, 0, (i, 1), (i - 1, 1))
                group(i, 1, (i + 1, 0), (i, 0))
            last = GROUPS // 2 - 1
            group(last, 0, (last, 1), (last - 1, 1))
            group(last, 1, None, (last, 0))
            turn_sums(last, 1, 1)
            spread_inverses(last, 1, 1)


def project_out_and_route(nc, t, wo):
    with ExitStack() as ctx:
        sb = lambda name, shape, dt=F32: ctx.enter_context(nc.sbuf_tensor(name, shape, dt))
        sem = lambda name: ctx.enter_context(nc.semaphore(name))
        psum = lambda name: ctx.enter_context(nc.psum_tensor(name, [P, 512], F32))
        wh, wl, bias3, ones = wo.high, wo.low, wo.bias, wo.ones
        gate = sb("d_gate", [P, KD, EXPERTS])
        ident = sb("d_ident", [P, P])
        eps = sb("d_eps", [P, 1])
        zero = sb("d_zero", [P, ROW])
        names = sb("d_names", [P, EXPERTS, CHOSEN])
        att = sb("d_att", [P, 2, KD, HALF])
        ah = sb("d_ah", [P, 2, KD, HALF], F32R)
        al = sb("d_al", [P, 2, KD, HALF], F32R)
        x = sb("d_x", [P, 2, 4, D])
        left = sb("d_left", [P, 2 * B, 4])
        xrow = sb("d_xrow", [P, 2, 4, D])
        gates = sb("d_gates", [P, 2, 4, EXPERTS])
        stats = sb("d_stats", [P, 4, 6])
        mv = sb("d_mv", [P, 4, 2])
        sd = sb("d_sd", [P, 4])
        rs = sb("d_rs", [P, 4])
        xt = sb("d_xt", [P, 2, KD, HALF])
        lt = sb("d_lt", [P, HALF])
        lg = sb("d_lg", [P, 4, EXPERTS])
        best = sb("d_best", [P, 4, 8])
        at = sb("d_at", [P, 4, 8], U32)
        nmax = sb("d_nmax", [P, 4])
        ex = sb("d_ex", [P, 4, EXPERTS])
        tot = sb("d_tot", [P, 4])
        itot = sb("d_itot", [P, 4])
        hit = sb("d_hit", [P, EXPERTS, CHOSEN])
        mask = sb("d_mask", [P, 4, EXPERTS])
        order = sb("d_order", [P, 4, EXPERTS])
        ordt = sb("d_ordt", [P, 2, HALF // 2])
        po = [psum(f"d_po{n}") for n in range(2)]
        pt = [psum(f"d_pt{n}") for n in range(2)]
        pg, pl, pk = psum("d_pg"), psum("d_pl"), psum("d_pk")
        consts, zeroed = sem("d_consts"), sem("d_zeroed")
        att_in = [sem(f"d_att_in{u}") for u in range(2)]
        x_in = [sem(f"d_x_in{u}") for u in range(2)]
        ah_done, al_done, projected, added, stat, aggregated = (sem(f"d_{n}") for n in ("ah_done", "al_done", "projected", "added", "stat", "aggregated"))
        rooted, inverted, normed, turned, xt_done = (sem(f"d_{n}") for n in ("rooted", "inverted", "normed", "turned", "xt_done"))
        gated, gate_out, lt_turned, ranked, nmax_done = (sem(f"d_{n}") for n in ("gated", "gate_out", "lt_turned", "ranked", "nmax_done"))
        exped, itot_done, masked, row_done, order_done = (sem(f"d_{n}") for n in ("exped", "itot_done", "masked", "row_done", "order_done"))
        order_turned, ordt_done, pad_stored = sem("d_order_turned"), sem("d_ordt_done"), sem("d_pad_stored")
        x1_stored = [sem(f"d_x1_stored{u}") for u in range(2)]
        row_stored = [sem(f"d_row_stored{u}") for u in range(2)]
        xt_stored = [sem(f"d_xt_stored{u}") for u in range(2)]
        gates_stored = [sem(f"d_gates_stored{u}") for u in range(2)]
        ord_stored = [sem(f"d_ord_stored{u}") for u in range(2)]
        block = ctx.enter_context(nc.Block())
        x_dram = t["x"].rearrange("b (u j p) d -> b u p j d", p=P, j=4)
        x1_dram = t["x1"].rearrange("(b u j p) d -> b u p j d", b=B, p=P, j=4)
        row_dram = t["xrow"][0:N].rearrange("(b u j p) d -> b u p j d", b=B, p=P, j=4)

        HALVES = 2 * B

        def before(b, u, d):
            return b + (u - d) // 2, (u - d) % 2

        def steps(step):
            for n in range(HALVES + 2):
                step(n // 2, n % 2, n)

        @block.sync
        def _(sp):
            def load_att(b, u):
                sp.dma_start(att[:, u], t["att"][b, :, :, u * HALF:(u + 1) * HALF].rearrange("g p s -> p g s")).then_inc(att_in[u], 16)

            def load_x(b, u):
                sp.dma_start(x[:, u], x_dram[b, u]).then_inc(x_in[u], 16)

            def step(b, u, n):
                tiles = 4 * n
                (b1, u1), (b2, u2) = before(b, u, 1), before(b, u, 2)
                if n + 2 < HALVES:
                    sp.wait_ge(al_done, n + 1)
                    load_att(b + 1, u)
                if 1 <= n <= HALVES:
                    sp.wait_ge(normed, tiles)
                    sp.dma_start(row_dram[b1, u1][:, :, 0:D], xrow[:, u1]).then_inc(row_stored[u1], 16)
                    sp.dma_start(x1_dram[b1, u1], x[:, u1]).then_inc(x1_stored[u1], 16)
                    if n + 1 < HALVES:
                        sp.wait_ge(x1_stored[u1], 16 * (b1 + 1))
                        load_x(b1 + 1, u1)
                    sp.wait_ge(xt_done, tiles)
                    sp.dma_start(t["xt2"][b1, u1], xt[:, u1]).then_inc(xt_stored[u1], 16)
                if n >= 2:
                    sp.wait_ge(row_done, tiles - 4)
                    sp.dma_start(row_dram[b2, u2][:, :, D:ROW], gates[:, u2]).then_inc(gates_stored[u2], 16)
                if n >= 2:
                    sp.wait_ge(ordt_done, n - 2 + 1)
                    for r in range(2):
                        sp.dma_start(t["order"][:, b2, u2].rearrange("e (j r p) -> r e j p", r=2, p=P)[r],
                                     ordt[r * EXPERTS:(r + 1) * EXPERTS, u2].rearrange("e (j p) -> e j p", p=P)).then_inc(ord_stored[u2], 16)

            load_att(0, 0)
            load_x(0, 0)
            load_att(0, 1)
            load_x(0, 1)
            sp.dma_start(gate[:], t["gate"].rearrange("(k p) n -> p k n", p=P)).then_inc(consts, 16)
            sp.dma_start(ident[:], t["ident"]).then_inc(consts, 16)
            sp.dma_start(names[:], t["expert_names"]).then_inc(consts, 16)
            sp.dma_start(left[:], t["left"].rearrange("b u p j -> p (b u) j")).then_inc(consts, 16)
            sp.wait_ge(zeroed, 3)
            sp.dma_start(t["xrow"][N:N + P], zero[:]).then_inc(pad_stored, 16)
            steps(step)
            sp.wait_ge(pad_stored, 16)
            for u in range(2):
                for stored in (x1_stored, row_stored, xt_stored, gates_stored):
                    sp.wait_ge(stored[u], 16 * B)
                sp.wait_ge(ord_stored[u], 32 * B)

        @block.vector
        def _(dve):
            nc.vector.memset(zero[:], 0.0).then_inc(zeroed, 1)
            nc.vector.memset(eps[:], EPS).then_inc(zeroed, 1)
            nc.vector.memset(lt[:], 0.0).then_inc(zeroed, 1)

            def split(b, u, n):
                dve.wait_ge(ah_done, n + 1)
                nc.vector.tensor_tensor(al[:, u], att[:, u], ah[:, u].bitcast(F32), ALU.subtract).then_inc(al_done, 1)

            def add(b, u, n, j):
                if j == 0:
                    dve.wait_ge(x_in[u], 16 * b + 16)
                dve.wait_ge(projected, 4 * n + j + 1)
                nc.vector.tensor_tensor(x[:, u, j], po[j % 2][:], x[:, u, j], ALU.add).then_inc(added, 1)
                dve.wait_ge(added, 4 * n + j + 1)
                nc.vector.bn_stats(stats[:, j], x[:, u, j]).then_inc(stat, 1)

            def normalise(b, u, n, first):
                dve.wait_ge(rooted, n + 1)
                nc.vector.reciprocal(rs[:], sd[:]).then_inc(inverted, 1)
                if not first:
                    dve.wait_ge(row_stored[u], 16 * b)
                dve.wait_ge(inverted, n + 1)
                for j in range(4):
                    nc.vector.tensor_scalar(xrow[:, u, j], x[:, u, j], mv[:, j, 0:1], rs[:, j:j + 1],
                                            ALU.subtract, ALU.mult).then_inc(normed, 1)

            def rank(b, u, n, first):
                dve.wait_ge(lt_turned, n + 1)
                if not first:
                    dve.wait_ge(row_done, 4 * n)
                    dve.wait_ge(order_turned, n)
                nc.vector.tensor_copy(lg[:], pl[:].rearrange("p (j e) -> p j e", j=4)[:, :, 0:EXPERTS]).then_inc(ranked, 1)
                dve.wait_ge(ranked, 1)
                for j in range(4):
                    nc.vector.max(best[:, j], lg[:, j]).then_inc(ranked, 1)
                for j in range(4):
                    dve.wait_ge(ranked, j + 2)
                    nc.vector.max_index(at[:, j], best[:, j], lg[:, j]).then_inc(ranked, 1)
                nc.vector.tensor_scalar(nmax[:], best[:, :, 0], -1.0, None, ALU.mult).then_inc(nmax_done, 1)
                for j in range(4):
                    dve.wait_ge(ranked, 9 + j)
                    nc.vector.tensor_tensor(hit[:], names[:], at[:, j, 0:CHOSEN].rearrange("p (o k) -> p o k", o=1).broadcast_to([P, EXPERTS, CHOSEN]),
                                            ALU.is_equal).then_inc(ranked, 1)
                    dve.wait_ge(ranked, 10 + j)
                    nc.vector.tensor_reduce(mask[:, j], hit[:], AX_X, ALU.add).then_inc(masked, 1)
                    dve.wait_ge(masked, 4 * n + j + 1)
                    nc.vector.tensor_scalar(order[:, j], mask[:, j], left[:, n, j:j + 1], None, ALU.mult).then_inc(order_done, 1)

            def gate_rows(b, u, n, first):
                dve.wait_ge(exped, 4 * n + 4)
                nc.vector.reciprocal(itot[:], tot[:]).then_inc(itot_done, 1)
                if not first:
                    dve.wait_ge(gates_stored[u], 16 * b)
                dve.wait_ge(itot_done, n + 1)
                for j in range(4):
                    nc.vector.scalar_tensor_tensor(out=gates[:, u, j], in0=ex[:, j], scalar=itot[:, j:j + 1], in1=mask[:, j],
                                                   op0=ALU.mult, op1=ALU.mult).then_inc(row_done, 1)

            def step(b, u, n):
                here = n < HALVES
                before1, before2 = before(b, u, 1), before(b, u, 2)
                dve.sem_clear(stat)
                dve.sem_clear(ranked)
                if 1 <= n <= HALVES:
                    dve.wait_ge(aggregated, 4 * n)
                    normalise(*before1, n - 1, n in (1, 2))
                    dve.wait_ge(normed, 4 * n)
                if here:
                    add(b, u, n, 0)
                if n >= 2:
                    rank(*before2, n - 2, n == 2)
                if here:
                    add(b, u, n, 1)
                    add(b, u, n, 2)
                if n + 1 < HALVES:
                    split(b + (u + 1) // 2, 1 - u, n + 1)
                if n >= 2:
                    gate_rows(*before2, n - 2, n in (2, 3))
                if here:
                    add(b, u, n, 3)
                    for j in range(4):
                        dve.wait_ge(stat, j + 1)
                        nc.vector.bn_aggr(mv[:, j], stats[:, j]).then_inc(aggregated, 1)

            split(0, 0, 0)
            dve.wait_ge(consts, 64)
            steps(step)

        @block.scalar
        def _(act):
            act.wait_ge(zeroed, 3)

            def split(b, u, n, first):
                act.wait_ge(att_in[u], 16 * b + 16)
                if not first:
                    act.wait_ge(projected, 4 * (n - 1))
                nc.scalar.copy(ah[:, u], att[:, u]).then_inc(ah_done, 1)

            def step(b, u, n):
                (b1, u1), (b2, u2) = before(b, u, 1), before(b, u, 2)
                if 1 <= n <= HALVES:
                    act.wait_ge(aggregated, 4 * (n - 1) + 4)
                    nc.scalar.activation(sd[:], mv[:, :, 1], ACT.Sqrt, bias=eps[:, 0:1]).then_inc(rooted, 1)
                    if n not in (1, 2):
                        act.wait_ge(xt_stored[u1], 16 * b1)
                    for k in range(KD):
                        act.wait_ge(turned, 4 * (n - 1) + k + 1)
                        nc.scalar.copy(xt[:, u1, k], pt[k % 2][:]).then_inc(xt_done, 1)
                if n >= 2:
                    act.wait_ge(nmax_done, n - 2 + 1)
                    for j in range(4):
                        nc.scalar.activation(ex[:, j], lg[:, j], ACT.Exp, bias=nmax[:, j:j + 1], accum_out=tot[:, j:j + 1]).then_inc(exped, 1)
                if n + 1 < HALVES:
                    split(b + (u + 1) // 2, 1 - u, n + 1, n == 0)
                if 1 <= n <= HALVES:
                    act.wait_ge(gated, n)
                    if n != 1:
                        act.wait_ge(lt_turned, n - 1)
                    nc.scalar.copy(lt[0:EXPERTS], pg[0:EXPERTS, :]).then_inc(gate_out, 1)
                if n >= 2:
                    act.wait_ge(order_turned, n - 2 + 1)
                    if n not in (2, 3):
                        act.wait_ge(ord_stored[u2], 32 * b2)
                    nc.scalar.copy(ordt[:, u2], pk[:, 0:HALF // 2]).then_inc(ordt_done, 1)

            split(0, 0, 0, True)
            steps(step)

        @block.tensor
        def _(pe):
            def project(u, n, j, first):
                if j == 0:
                    pe.wait_ge(al_done, n + 1)
                if not (first and j < 2):
                    pe.wait_ge(added, 4 * n + j - 1)
                rows = slice(j * P, (j + 1) * P)
                nc.tensor.matmul(po[j % 2][:], ones[:], bias3[:], start=True, stop=False)
                for k in range(KD):
                    nc.tensor.matmul(po[j % 2][:], ah[:, u, k, rows], wh[:, k], start=False, stop=False)
                    nc.tensor.matmul(po[j % 2][:], ah[:, u, k, rows], wl[:, k], start=False, stop=False)
                    last = nc.tensor.matmul(po[j % 2][:], al[:, u, k, rows], wh[:, k], start=False, stop=(k == KD - 1))
                last.then_inc(projected, 1)

            def step(b, u, n):
                here = n < HALVES
                one = 1 <= n <= HALVES
                u1 = 1 - u
                if here:
                    project(u, n, 0, n == 0)
                    project(u, n, 1, n == 0)
                if one:
                    if n == 1:
                        pe.wait_ge(consts, 64)
                    pe.wait_ge(normed, 4 * (n - 1) + 4)
                    for k in range(KD):
                        if not (n == 1 and k < 2):
                            pe.wait_ge(xt_done, 4 * (n - 1) + k - 1)
                        for j in range(4):
                            last = nc.tensor.transpose(pt[k % 2][:, j * P:(j + 1) * P], xrow[:, u1, j, k * P:(k + 1) * P], ident[:])
                        last.then_inc(turned, 1)
                if here:
                    project(u, n, 2, False)
                if one:
                    if n != 1:
                        pe.wait_ge(gate_out, n - 1)
                    for k in range(KD):
                        pe.wait_ge(xt_done, 4 * (n - 1) + k + 1)
                        last = nc.tensor.matmul(pg[0:EXPERTS, :], gate[:, k], xt[:, u1, k], start=(k == 0), stop=(k == KD - 1))
                    last.then_inc(gated, 1)
                if here:
                    project(u, n, 3, False)
                if n >= 2:
                    pe.wait_ge(order_done, 4 * (n - 2) + 4)
                    if n != 2:
                        pe.wait_ge(ordt_done, n - 2)
                    for j in range(2):
                        last = nc.tensor.transpose(pk[:, j * P:(j + 1) * P], order[:, 2 * j:2 * j + 2].rearrange("p j e -> p (j e)"), ident[:])
                    last.then_inc(order_turned, 1)
                if one:
                    if n != 1:
                        pe.wait_ge(nmax_done, n - 1)
                    pe.wait_ge(gate_out, n)
                    for j in range(4):
                        last = nc.tensor.transpose(pl[:, j * P:(j + 1) * P], lt[:, j * P:(j + 1) * P], ident[:])
                    last.then_inc(lt_turned, 1)

            steps(step)


def shared_experts(nc, t):
    CH = SHARED_CHUNKS
    HALVES = 2 * B
    PIECES = 2
    WHOLE = (CH - 1) * P
    REST = SHARED - WHOLE
    with ExitStack() as ctx:
        sb = lambda name, shape, dt=F32: ctx.enter_context(nc.sbuf_tensor(name, shape, dt))
        sem = lambda name: ctx.enter_context(nc.semaphore(name))
        psum = lambda name: ctx.enter_context(nc.psum_tensor(name, [P, 512], F32))
        raw = sb("e_raw", [P, CH * D])
        up = [sb(f"e_sw13{part}", [P, KD, 2 * SHARED], F32R) for part in "hl"]
        down = [sb(f"e_sw2{part}", [P, CH, D], F32R) for part in "hl"]
        x = sb("e_x", [P, KD, HALF])
        xh = sb("e_xh", [P, 2, KD, HALF], F32R)
        xl = sb("e_xl", [P, 2, KD, HALF], F32R)
        silu = sb("e_silu", [P, 2, HALF])
        h = sb("e_h", [P, 2, HALF])
        hh = sb("e_hh", [P, 3, HALF], F32R)
        hl = sb("e_hl", [P, 3, HALF], F32R)
        shared = sb("e_shared", [P, 8, D])
        z, x1 = shared[:, 0:4], shared[:, 4:8]
        raw3 = shared[:, 0:CH].rearrange("p a b -> p (a b)")
        order = sb("e_order", [EXPERTS, N])
        top = sb("e_top", [EXPERTS, 8])
        first = sb("e_first", [EXPERTS, CAPACITY])
        p1 = [psum(f"e_p1{n}") for n in range(2)]
        p3 = [psum(f"e_p3{n}") for n in range(2)]
        pz = [psum(f"e_pz{n}") for n in range(4)]
        raw_in = [sem(f"e_raw_in{n}") for n in range(3)]
        split_h, split_l = sem("e_split_h"), sem("e_split_l")
        x_in, x1_in, xh_done, xl_done = sem("e_x_in"), sem("e_x1_in"), sem("e_xh_done"), sem("e_xl_done")
        up_done, silu_done, h_done, hh_done, hl_done, down_done = (
            sem(f"e_{n}") for n in ("up_done", "silu_done", "h_done", "hh_done", "hl_done", "down_done"))
        summed, stored = sem("e_summed"), sem("e_stored")
        order_in, ranked, list_stored = (sem(f"e_{n}") for n in ("order_in", "ranked", "list_stored"))
        block = ctx.enter_context(nc.Block())
        xt2 = t["xt2"].rearrange("b u p k s -> (b u) p k s")
        x1_dram = t["x1"].rearrange("(n j p) d -> n p j d", p=P, j=4)
        out_dram = t["out"][0:N].rearrange("(n j p) d -> n p j d", p=P, j=4)

        def piece(n, c):
            raws = (raw[:], raw3, raw[:])[n]
            if n < 2:
                ks, cols = slice(c * KD // PIECES, (c + 1) * KD // PIECES), slice(n * SHARED, (n + 1) * SHARED)
                return up[0][:, ks, cols], up[1][:, ks, cols], raws[:, 0:KD * SHARED].rearrange("p (k n) -> p k n", k=KD)[:, ks]
            ks = slice(c * CH // PIECES, (c + 1) * CH // PIECES)
            return down[0][:, ks], down[1][:, ks], raws.rearrange("p (k n) -> p k n", k=CH)[:, ks]

        def halves(engine, body):
            for u in range(2):
                body(u, u, u == 0, False)
            with engine.Fori(1, HALVES // 2 - 1) as i:
                for u in range(2):
                    body(2 * i + u, u, False, False)
            for u in range(2):
                body(HALVES - 2 + u, u, False, u == 1)

        @block.sync
        def _(sp):
            def load_weight(n):
                if n < 2:
                    to = (raw[:], raw3)[n][:, 0:KD * SHARED].rearrange("p (k n) -> p k n", k=KD)
                    come = t["sw13"][:, n * SHARED:(n + 1) * SHARED].rearrange("(k p) n -> p k n", p=P)
                else:
                    to, come = raw[:].rearrange("p (k n) -> p k n", k=CH), t["sw2"].rearrange("(k p) n -> p k n", p=P)
                sp.dma_start(to, come).then_inc(raw_in[n], 16)

            def finish(n):
                sp.wait_ge(summed, 4 * n + 4)
                sp.dma_start(out_dram[n], z).then_inc(stored, 16)

            def body(n, u, early, last):
                if not last:
                    sp.wait_ge(xl_done, KD * n + KD)
                    sp.dma_start(x[:], xt2[n + 1]).then_inc(x_in, 16)
                if not early:
                    finish(n - 1)
                    sp.dma_start(x1, x1_dram[n]).then_inc(x1_in, 16)

            load_weight(0)
            sp.dma_start(x[:], xt2[0]).then_inc(x_in, 16)
            load_weight(1)
            sp.wait_ge(split_l, PIECES)
            load_weight(2)
            sp.dma_start(order[:], t["order"].rearrange("e b u s -> e (b u s)")).then_inc(order_in, 16)
            sp.wait_ge(split_l, 2 * PIECES)
            sp.dma_start(x1, x1_dram[0]).then_inc(x1_in, 16)
            halves(sp, body)
            finish(HALVES - 1)
            sp.wait_ge(ranked, 3)
            sp.dma_start(t["first"], first[:]).then_inc(list_stored, 16)
            sp.wait_ge(stored, 16 * HALVES)
            sp.wait_ge(list_stored, 16)

        @block.vector
        def _(dve):
            def find(early):
                if early:
                    dve.wait_ge(order_in, 16)
                else:
                    dve.wait_ge(ranked, 3)
                dve.sem_clear(ranked)
                nc.vector.max(top[:], order[:]).then_inc(ranked, 1)

            def strike(r):
                dve.wait_ge(ranked, 1)
                nc.vector.match_replace(order[:], top[:], order[:], 0.0).then_inc(ranked, 1)
                nc.vector.tensor_copy(first[:, bass.ds(8 * r, 8)], top[:]).then_inc(ranked, 1)

            def add(n, early):
                dve.wait_ge(down_done, CH * n + CH)
                dve.wait_ge(x1_in, 16 * n + 16)
                if not early:
                    dve.wait_ge(stored, 16 * n)
                for j in range(4):
                    nc.vector.tensor_tensor(z[:, j], pz[j][:], x1[:, j], ALU.add).then_inc(summed, 1)

            def body(n, u, early, last):
                for m in range(CH):
                    at = CH * n + m
                    if m == 2 and not early:
                        add(n - 1, isinstance(n, int) and n == 1)
                    dve.wait_ge(silu_done, at + 1)
                    dve.wait_ge(up_done, 2 * at + 2)
                    if not (early and m < 2):
                        dve.wait_ge(hl_done, at - 1)
                    if m < CH - 1:
                        nc.vector.tensor_tensor(h[:, m % 2], silu[:, m % 2], p3[m % 2][:], ALU.mult).then_inc(h_done, 1)
                    else:
                        nc.vector.tensor_tensor(h[0:REST, m % 2], silu[0:REST, m % 2], p1[m % 2][REST:2 * REST, :], ALU.mult).then_inc(h_done, 1)
                    if m in (0, 3):
                        find(early and m == 0)
                    elif m in (1, 4):
                        strike(2 * n + m // 3)

            for n in range(3):
                for c in range(PIECES):
                    high, low, src = piece(n, c)
                    dve.wait_ge(split_h, PIECES * n + c + 1)
                    nc.vector.tensor_tensor(low, src, high.bitcast(F32), ALU.subtract).then_inc(split_l, 1)
            halves(dve, body)
            add(HALVES - 1, False)

        @block.scalar
        def _(act):
            def split(n, u, k):
                if k == 0:
                    act.wait_ge(x_in, 16 * n + 16)
                nc.scalar.copy(xh[:, u, k], x[:, k]).then_inc(xh_done, 1)

            def body(n, u, early, last):
                for m in range(CH):
                    at = CH * n + m
                    act.wait_ge(up_done, 2 * at + 1)
                    rows = slice(0, P if m < CH - 1 else REST)
                    nc.scalar.activation(silu[rows, m % 2], p1[m % 2][rows, :], ACT.Silu).then_inc(silu_done, 1)
                    if m >= 1 and m <= KD and not last:
                        split(n + 1, 1 - u, m - 1)
                    act.wait_ge(h_done, at + 1)
                    if not (early and m < 3):
                        act.wait_ge(down_done, at - 2)
                    nc.scalar.copy(hh[:, m % 3], h[:, m % 2]).then_inc(hh_done, 1)

            for n in range(3):
                act.wait_ge(raw_in[n], 16)
                for c in range(PIECES):
                    high, low, src = piece(n, c)
                    nc.scalar.copy(high, src).then_inc(split_h, 1)
                if n == 0:
                    for k in range(KD):
                        split(0, 0, k)
            halves(act, body)

        @block.gpsimd
        def _(pool):
            def split(n, u, k):
                pool.wait_ge(xh_done, KD * n + k + 1)
                nc.gpsimd.tensor_tensor(xl[:, u, k], x[:, k], xh[:, u, k].bitcast(F32), ALU.subtract).then_inc(xl_done, 1)

            def body(n, u, early, last):
                for m in range(CH):
                    at = CH * n + m
                    if m >= 1 and m <= KD and not last:
                        split(n + 1, 1 - u, m - 1)
                    pool.wait_ge(hh_done, at + 1)
                    nc.gpsimd.tensor_tensor(hl[:, m % 3], h[:, m % 2], hh[:, m % 3].bitcast(F32), ALU.subtract).then_inc(hl_done, 1)

            for k in range(KD):
                split(0, 0, k)
            halves(pool, body)

        @block.tensor
        def _(pe):
            def rise(n, u, m, early):
                at = CH * n + m
                if m == 0:
                    pe.wait_ge(xl_done, KD * n + KD)
                if not (early and m < 2):
                    pe.wait_ge(h_done, at - 1)
                if m < CH - 1:
                    products = ((p1[m % 2], m * P), (p3[m % 2], WHOLE + m * P))
                else:
                    products = ((p1[m % 2], 2 * WHOLE),)
                for r, (bank, first_col) in enumerate(products):
                    if early and m == 0:
                        pe.wait_ge(split_l, PIECES * (r + 1))
                    cols = slice(first_col, first_col + P)
                    for k in range(KD):
                        nc.tensor.matmul(bank[:], up[0][:, k, cols], xh[:, u, k], start=(k == 0), stop=False)
                        nc.tensor.matmul(bank[:], up[0][:, k, cols], xl[:, u, k], start=False, stop=False)
                        last = nc.tensor.matmul(bank[:], up[1][:, k, cols], xh[:, u, k], start=False, stop=(k == KD - 1))
                    last.then_inc(up_done, 2 // len(products))

            def fall(n, m, early):
                at = CH * n + m
                if early and m == 0:
                    pe.wait_ge(split_l, 3 * PIECES)
                pe.wait_ge(hl_done, at + 1)
                for j in range(4):
                    if m == 0 and not early:
                        pe.wait_ge(summed, 4 * n + j - 3)
                    rows = slice(j * P, (j + 1) * P)
                    nc.tensor.matmul(pz[j][:], hh[:, m % 3, rows], down[0][:, m], start=(m == 0), stop=False)
                    nc.tensor.matmul(pz[j][:], hh[:, m % 3, rows], down[1][:, m], start=False, stop=False)
                    last = nc.tensor.matmul(pz[j][:], hl[:, m % 3, rows], down[0][:, m], start=False, stop=(m == CH - 1))
                last.then_inc(down_done, 1)

            def body(n, u, early, last):
                for m in range(CH):
                    rise(n, u, m, early)
                    if m >= 2:
                        fall(n, m - 2, early)
                    elif not early:
                        fall(n - 1, CH - 2 + m, False)

            halves(pe, body)
            fall(HALVES - 1, CH - 2, False)
            fall(HALVES - 1, CH - 1, False)


def routed_experts(nc, t):
    TURN = 4
    CHUNKS = [(0, P), (P, P), (2 * P, INTER - 2 * P)]
    LAST = INTER - 2 * P
    TURNS = EXPERTS // TURN
    with ExitStack() as ctx:
        sb = lambda name, shape, dt=F32: ctx.enter_context(nc.sbuf_tensor(name, shape, dt))
        sem = lambda name: ctx.enter_context(nc.semaphore(name))
        psum = lambda name: ctx.enter_context(nc.psum_tensor(name, [P, 512], F32))
        w13 = sb("r_w13", [P, TURN, KD, 2 * INTER])
        w2 = sb("r_w2", [P, TURN, 3, D])
        ident = sb("r_ident", [P, P])
        slot = sb("r_slot", [P, 1])
        first = sb("r_first", [EXPERTS, CAPACITY])
        empty = sb("r_empty", [P, EXPERTS])
        row = sb("r_row", [P, EXPERTS])
        zero = sb("r_zero", [P, D])
        picked = sb("r_picked", [P, TURN], U32)
        added_to = sb("r_added_to", [P, TURN], U32)
        xe = sb("r_xe", [P, TURN, ROW])
        xt = sb("r_xt", [P, 2, KD * P])
        silu = sb("r_silu", [P, 2, 3 * P])
        h = sb("r_h", [P, 2, 3 * P])
        y = sb("r_y", [P, 2, D])
        p1 = [psum(f"r_p1{n}") for n in range(2)]
        p3 = [psum(f"r_p3{n}") for n in range(2)]
        pt = [psum(f"r_pt{n}") for n in range(2)]
        py = [psum(f"r_py{n}") for n in range(2)]
        consts, zero_set, zero_out, first_turned, rows_found = (sem(f"r_{n}") for n in ("consts", "zero_set", "zero_out", "first_turned", "rows_found"))
        w_in = [sem(f"r_w_in{s}") for s in range(TURN)]
        gathered = [sem(f"r_gathered{s}") for s in range(TURN)]
        picked_done = [sem(f"r_picked_done{s}") for s in range(TURN)]
        scaled = [sem(f"r_scaled{s}") for s in range(TURN)]
        turned, xt_done, up_done = (sem(f"r_{n}") for n in ("turned", "xt_done", "up_done"))
        silu_done, h_done, down_done, scattered, added = (sem(f"r_{n}") for n in ("silu_done", "h_done", "down_done", "scattered", "added"))
        block = ctx.enter_context(nc.Block())

        def turns(engine, body):
            body(0, 0)
            with engine.Fori(1, TURNS - 1) as i:
                body(i, None)
            body(TURNS - 1, EXPERTS - TURN)

        @block.sync
        def _(sp):
            sp.dma_start(first[:], t["first"]).then_inc(consts, 16)
            sp.dma_start(ident[:], t["ident"]).then_inc(consts, 16)
            sp.dma_start(slot[:], t["slot"]).then_inc(consts, 16)

            def load(i, s):
                e = TURN * i + s
                sp.dma_start(w13[:, s], t["w13"][e]).then_inc(w_in[s], 16)
                sp.dma_start(w2[:, s, 0:2], t["w2"][e, 0:2 * P].rearrange("(c p) d -> p c d", p=P)).then_inc(w_in[s], 16)
                sp.dma_start(w2[0:LAST, s, 2], t["w2"][e, 2 * P:INTER]).then_inc(w_in[s], 16)

            load(0, 0)
            sp.wait_ge(zero_set, 1)
            sp.dma_start(t["out"][N:N + P], zero[:]).then_inc(zero_out, 16)
            sp.wait_ge(gathered[0], 16)
            for s in range(1, TURN):
                load(0, s)
            with sp.Fori(1, TURNS) as i:
                for s in range(TURN):
                    sp.wait_ge(down_done, TURN * (i - 1) + s + 1)
                    load(i, s)
            sp.wait_ge(zero_out, 16)

        @block.gpsimd
        def _(pool):
            nc.gpsimd.memset(zero[:], 0.0).then_inc(zero_set, 1)

            def gather(e, s):
                pool.wait_ge(picked_done[s], 1)
                pool.sem_clear(picked_done[s])
                nc.gpsimd.indirect_dma_start(xe[:, s], None, t["xrow"], bass.IndirectOffsetOnAxis(picked[:, s:s + 1], 0)).then_inc(gathered[s], 16)

            def add_done(e):
                pool.wait_ge(scattered, 16 * (e + 1))
                pool.sem_inc(added, 1)

            def scatter(e, s, first):
                pool.wait_ge(scaled[s], 2)
                pool.sem_clear(scaled[s])
                if not first:
                    add_done(e - 1)
                nc.gpsimd.indirect_dma_start(t["out"], bass.IndirectOffsetOnAxis(added_to[:, s:s + 1], 0), y[:, s % 2], None, compute_op=ALU.add).then_inc(scattered, 16)

            def body(i, at):
                for s in range(TURN):
                    e = TURN * i + s
                    if at is None or at + s > 0:
                        scatter(e - 1, (s - 1) % TURN, at == 0 and s == 1)
                    if at is None or at + s + 3 < EXPERTS:
                        gather(e + 3, (s + 3) % TURN)

            for s in range(3):
                gather(s, s)
            pool.wait_ge(zero_out, 16)
            turns(pool, body)
            scatter(EXPERTS - 1, TURN - 1, False)
            add_done(EXPERTS - 1)

        @block.vector
        def _(dve):
            dve.wait_ge(first_turned, 1)
            nc.vector.tensor_scalar(empty[:], p1[0][:, 0:EXPERTS], 0.0, slot[:, 0:1], ALU.is_equal, ALU.mult).then_inc(rows_found, 1)
            nc.vector.tensor_scalar(row[:], p1[0][:, 0:EXPERTS], -1.0, float(N), ALU.mult, ALU.add).then_inc(rows_found, 1)
            dve.wait_ge(rows_found, 2)
            nc.vector.tensor_tensor(row[:], row[:], empty[:], ALU.add).then_inc(rows_found, 1)
            dve.wait_ge(rows_found, 3)

            def pick(e, s, i, first):
                if not first:
                    dve.wait_ge(gathered[s], 16 * i)
                nc.vector.tensor_scalar(picked[:, s:s + 1], row[:, bass.ds(e, 1)], 1.0, None, ALU.mult).then_inc(picked_done[s], 1)

            def multiply(e, s, first):
                b = s % 2
                dve.wait_ge(silu_done, 2 * e + 2)
                if not first:
                    dve.wait_ge(down_done, e - 1)
                nc.vector.tensor_tensor(h[:, b, 0:2 * P], silu[:, b, 0:2 * P], p3[b][:, 0:2 * P], ALU.mult).then_inc(h_done, 1)
                nc.vector.tensor_tensor(h[0:LAST, b, 2 * P:], silu[0:LAST, b, 2 * P:], p3[b][0:LAST, 2 * P:3 * P], ALU.mult).then_inc(h_done, 1)

            def scale(e, s, first):
                dve.wait_ge(down_done, e + 1)
                if not first:
                    dve.wait_ge(added, e - 1)
                nc.vector.tensor_scalar(added_to[:, s:s + 1], row[:, bass.ds(e, 1)], 1.0, None, ALU.mult).then_inc(scaled[s], 1)
                nc.vector.tensor_scalar(y[:, s % 2], py[s % 2][:], xe[:, s, bass.ds(e + D, 1)], None, ALU.mult).then_inc(scaled[s], 1)

            def body(i, at):
                for s in range(TURN):
                    e = TURN * i + s
                    multiply(e, s, at == 0 and s < 2)
                    if at is None or at + s > 0:
                        scale(e - 1, (s - 1) % TURN, at == 0 and s - 1 < 2)
                    if at is None or at + s + 3 < EXPERTS:
                        pick(e + 3, (s + 3) % TURN, i + (s + 3) // TURN, at == 0 and s == 0)

            for s in range(3):
                pick(s, s, 0, True)
            turns(dve, body)
            scale(EXPERTS - 1, TURN - 1, False)

        @block.scalar
        def _(act):
            def body(i, at):
                for s in range(TURN):
                    e = TURN * i + s
                    b = s % 2
                    act.wait_ge(up_done, e + 1)
                    if not (at == 0 and s < 2):
                        act.wait_ge(h_done, 2 * e - 2)
                    nc.scalar.activation(silu[:, b, 0:2 * P], p1[b][:, 0:2 * P], ACT.Silu).then_inc(silu_done, 1)
                    nc.scalar.activation(silu[0:LAST, b, 2 * P:], p1[b][0:LAST, 2 * P:3 * P], ACT.Silu).then_inc(silu_done, 1)
                    if at is None or at + s + 1 < EXPERTS:
                        act.wait_ge(turned, e + 2)
                        nc.scalar.copy(xt[:, 1 - b], pt[1 - b][:]).then_inc(xt_done, 1)

            act.wait_ge(turned, 1)
            nc.scalar.copy(xt[:, 0], pt[0][:]).then_inc(xt_done, 1)
            turns(act, body)

        @block.tensor
        def _(pe):
            pe.wait_ge(consts, 48)
            nc.tensor.transpose(p1[0][:, 0:EXPERTS], first[:], ident[0:EXPERTS, 0:EXPERTS]).then_inc(first_turned, 1)
            pe.wait_ge(rows_found, 2)

            def turn(e, s, i, first):
                pe.wait_ge(gathered[s], 16 * i + 16)
                if not first:
                    pe.wait_ge(xt_done, e - 1)
                for k in range(KD):
                    last = nc.tensor.transpose(pt[s % 2][:, k * P:(k + 1) * P], xe[:, s, k * P:(k + 1) * P], ident[:])
                last.then_inc(turned, 1)

            def rise(e, s, i, first):
                b = s % 2
                pe.wait_ge(xt_done, e + 1)
                pe.wait_ge(w_in[s], 48 * i + 48)
                if not first:
                    pe.wait_ge(h_done, 2 * e - 2)
                for bank, start in ((p1[b], 0), (p3[b], INTER)):
                    for c, (at, size) in enumerate(CHUNKS):
                        for k in range(KD):
                            last = nc.tensor.matmul(bank[0:size, c * P:(c + 1) * P], w13[:, s, k, start + at:start + at + size], xt[:, b, k * P:(k + 1) * P],
                                                    start=(k == 0), stop=(k == KD - 1))
                last.then_inc(up_done, 1)

            def fall(e, s, first):
                b = s % 2
                pe.wait_ge(h_done, 2 * e + 2)
                for c, (at, size) in enumerate(CHUNKS):
                    last = nc.tensor.matmul(py[b][:], h[0:size, b, c * P:(c + 1) * P], w2[0:size, s, c], start=(c == 0), stop=(c == 2))
                last.then_inc(down_done, 1)

            def body(i, at):
                for s in range(TURN):
                    e = TURN * i + s
                    rise(e, s, i, at == 0 and s < 2)
                    if at is None or at + s + 1 < EXPERTS:
                        turn(e + 1, (s + 1) % TURN, i + (s + 1) // TURN, at == 0 and s + 1 < 2)
                    if at is None or at + s > 0:
                        fall(e - 1, (s - 1) % TURN, at == 0 and s - 1 < 2)

            turn(0, 0, 0, True)
            turns(pe, body)
            fall(EXPERTS - 1, TURN - 1, False)


def clear_semaphores(nc, used):
    with nc.Block() as block:

        @block.vector
        def _(dve):
            for semaphore in used:
                dve.sem_clear(semaphore)


def decoder_layer_kernel(nc, t):
    for name, shape, dtype in (
        ("xnt", (2 * B, P, KD, HALF), F32),
        ("lg", (B, HEADS, S), F32),
        ("qh", (B, 4, S // P, P, P), F32),
        ("ql", (B, 4, S // P, P, P), F32),
        ("kv", (N * KV_HEADS, P), F32),
        ("keys", (B * HEADS, -(-TOPK // 8) * 8), U32),
        ("att", (B, 4, P, S), F32),
        ("x1", (N, D), F32),
        ("xrow", (N + P, ROW), F32),
        ("xt2", (B, 2, P, KD, HALF), F32),
        ("order", (EXPERTS, B, 2, HALF), F32),
        ("first", (EXPERTS, CAPACITY), F32),
    ):
        t[name] = nc.dram_tensor(f"{name}_scratch", shape, dtype).ap()
    with ExitStack() as ctx:
        qkv = Projection(nc, ctx, "qkv", 2 * D)
        clear_semaphores(nc, normalise_and_route(nc, t, qkv))
        project_and_rank(nc, t, qkv)
    with ExitStack() as ctx:
        wo = Projection(nc, ctx, "wo", D)
        attend(nc, t, wo)
        project_out_and_route(nc, t, wo)
    shared_experts(nc, t)
    routed_experts(nc, t)


def rotary_tables():
    import numpy as np

    pos = np.arange(S, dtype=np.float32)
    inv_freq = np.float32(1.0) / np.float32(1000000.0) ** (np.arange(0, DH, 2, dtype=np.float32) / np.float32(DH))
    freqs = pos[:, None] * inv_freq[None, :]
    cos, sin = np.cos(freqs), np.sin(freqs)
    both = np.stack([np.concatenate([cos, cos], -1), np.concatenate([sin, -sin], -1)], 1)
    return both.reshape(S // P, P, 2, DH).astype(np.float32)


def key_row_picks():
    import numpy as np

    full = TOPK // P * P
    padded = -(-TOPK // 8) * 8
    picks = np.zeros((DH, 4, 640), np.float32)
    for j in range(4):
        picks[2 * j:2 * j + 2, j, 0:full] = 1.0
        picks[2 * j:2 * j + 2, j, padded + DH * j:padded + DH * (j + 1)] = 1.0
    return picks


def kernel(**inputs):
    import numpy as np
    import concourse.bacc as _bacc
    from concourse import mybir as _mybir
    from concourse.bass_utils import run_bass_kernel_spmd as _run

    attn = lambda name: np.asarray(inputs[f"L0_attn_{name}"])
    ffn = lambda name: np.asarray(inputs[f"L0_ffn_{name}"])

    def chunked(w):
        return w.reshape(EXPERTS, INTER, KD, P).transpose(0, 3, 2, 1)

    wide = SHARED_CHUNKS * P - SHARED
    whole = (SHARED_CHUNKS - 1) * P
    tokens = np.arange(N, dtype=np.float32)
    arrays = {
        "x": attn("hidden_states"),
        "wr": attn("Wr"), "br": attn("br"),
        "wq": attn("Wq"), "wk": attn("Wk"), "wv": attn("Wv"),
        "bq": attn("bq"), "bk": attn("bk"), "bv": attn("bv"),
        "wo": attn("Wo"), "bo": attn("bo"),
        "gate": ffn("gate_w").T,
        "sw13": np.concatenate([ffn("sw1").T[:, :whole], ffn("sw3").T[:, :whole], ffn("sw1").T[:, whole:], ffn("sw3").T[:, whole:]], 1),
        "sw2": np.pad(ffn("sw2").T, ((0, wide), (0, 0))),
        "w13": np.concatenate([chunked(ffn("w1")), chunked(ffn("w3"))], -1),
        "w2": ffn("w2").transpose(0, 2, 1),
        "ident": np.eye(P, dtype=np.float32),
        "cs": rotary_tables(),
        "kv_base": np.array([[b * S * KV_HEADS + h * KV_HEADS // HEADS] for b in range(B) for h in range(HEADS)], np.float32),
        "pick_rows": key_row_picks(),
        "expert_names": np.broadcast_to(np.arange(EXPERTS, dtype=np.float32)[None, :, None], (P, EXPERTS, CHOSEN)),
        "left": (N - tokens).reshape(B, 2, HALF // P, P).transpose(0, 1, 3, 2),
        "slot": np.arange(CAPACITY, dtype=np.float32)[:, None],
    }
    arrays = {name: np.ascontiguousarray(a) for name, a in arrays.items()}
    nc = _bacc.Bacc("TRN2", target_bir_lowering=False, num_devices=1)
    t = {name: nc.dram_tensor(name, a.shape, _mybir.dt.from_np(a.dtype), kind="ExternalInput").ap() for name, a in arrays.items()}
    t["out"] = nc.dram_tensor("out", (N + P, D), _mybir.dt.float32, kind="ExternalOutput").ap()
    decoder_layer_kernel(nc, t)
    got = _run(nc, [arrays], core_ids=[0])
    return got.results[0]["out"][:N].reshape(B, S, D)
```
